# Optimizing a Trainium2 kernel written in Bass

```python
import numpy as np
import jax
import jax.numpy as jnp

def _softmax(x, axis=-1):
    return jax.nn.softmax(x, axis=axis)

def _gelu(x):
    return jax.nn.gelu(x, approximate=True)

def _silu(x):
    return jax.nn.silu(x)

def _sigmoid(x):
    return jax.nn.sigmoid(x)

def _layernorm(x, axis=-1, eps=1e-05):
    m = jnp.mean(x, axis=axis, keepdims=True)
    v = jnp.var(x, axis=axis, keepdims=True)
    return (x - m) / jnp.sqrt(v + eps)

def _scatter_add(tgt, idx, src, axis=0):
    return tgt.at[idx].add(src)

def _segment_sum(src, seg, n):
    return jax.ops.segment_sum(src, seg, n)
kernel_name = 'mk_flamingo_gated_d1_seqx_r8_35eb1a'

def setup_inputs(seed: int=0):
    np.random.seed(seed)
    _w = jnp.asarray

    def _rec_inputs():
        import jax
        import jax.numpy as jnp
        _rk = jax.random.key(seed)
        x = -0.0002928 + 1 * jax.random.normal(jax.random.fold_in(_rk, 1), (32, 128, 128), jnp.float32)
        _lenS = 128 - jax.random.randint(jax.random.fold_in(_rk, 7), (32,), 0, max(1, 128 // 4) + 1, jnp.int32)
        _lenS2 = 128 - jax.random.randint(jax.random.fold_in(_rk, 8), (32,), 0, max(1, 128 // 4) + 1, jnp.int32)
        _ctx_1024P = jax.random.normal(jax.random.fold_in(_rk, 11), (32, 16, 128), jnp.float32)
        _ctx_1024c = jax.random.dirichlet(jax.random.fold_in(_rk, 511), 0.3 * jnp.ones((16,), jnp.float32), (32, 128))
        _ctx_1024t = jnp.einsum('bsk,bkd->bsd', _ctx_1024c, _ctx_1024P)
        _ctx_1024t = _ctx_1024t * jax.lax.rsqrt(jnp.mean(jnp.square(_ctx_1024t)) + 1e-12) * 0.953939
        ctx_1024 = -1.39393e-06 + 0.999914 * (_ctx_1024t + 0.3 * jax.random.normal(jax.random.fold_in(_rk, 611), (32, 128, 128), jnp.float32))
        _g = jax.random.normal(jax.random.fold_in(_rk, 9001), (2, 1), jnp.float32)
        _g = jnp.sign(_g) * jnp.maximum(jnp.abs(_g), 1.0) + (_g == 0) * 1.0
        g_xattn = _g[0]
        g_ffn = _g[1]
        return (x, ctx_1024, g_xattn, g_ffn)
    x, ctx_1024, g_xattn, g_ffn = _rec_inputs()

    def _L0_xattn_setup():
        import jax, jax.numpy as jnp
        import numpy as np
        NUM_HEADS = 16
        key = jax.random.key(seed)
        kq, kk, kv = jax.random.split(key, 3)
        B, S, DIM = (2, 256, 128)
        q = jax.random.normal(kq, (B, S, DIM), dtype=jnp.float32)
        k = jax.random.normal(kk, (B, S, DIM), dtype=jnp.float32)
        v = jax.random.normal(kv, (B, S, DIM), dtype=jnp.float32)
        return {'q': q, 'k': k, 'v': v}
    _L0_xattn_all = _L0_xattn_setup()
    _L0_xattn_in = {k: v for k, v in _L0_xattn_all.items() if k in ()}
    del _L0_xattn_all

    def _L0_ffn_setup():
        import jax, jax.numpy as jnp
        import numpy as np
        NUM_HEADS = 16
        TOP_K = 2
        ROPE_BASE = 10000.0
        LN_EPS = 1e-05

        def _rope_sin_cos(S, D, dtype):
            inv_freq = 1.0 / ROPE_BASE ** (jnp.arange(0, D, 2, dtype=jnp.float32) / D)
            freqs = jnp.arange(S, dtype=jnp.float32)[:, None] * inv_freq[None, :]
            sin = jnp.sin(freqs).astype(dtype)[None, :, None, :]
            cos = jnp.cos(freqs).astype(dtype)[None, :, None, :]
            return (sin, cos)

        def _apply_rope(x, sin, cos):
            x1, x2 = (x[..., 0::2], x[..., 1::2])
            r1 = x1 * cos - x2 * sin
            r2 = x1 * sin + x2 * cos
            return jnp.stack([r1, r2], axis=-1).reshape(x.shape)

        def _layer_norm(x, w, b):
            mu = jnp.mean(x, axis=-1, keepdims=True)
            var = jnp.mean(jnp.square(x - mu), axis=-1, keepdims=True)
            return (x - mu) * jax.lax.rsqrt(var + LN_EPS) * w + b
        key = jax.random.key(seed)
        ks = jax.random.split(key, 8)
        B, S, E, NE = (2, 256, 128, 8)
        s = 0.02
        return {'x': jax.random.normal(ks[0], (B, S, E), dtype=jnp.float32), 'in_proj_w': jax.random.normal(ks[1], (3 * E, E), dtype=jnp.float32) * s, 'in_proj_b': jnp.zeros((3 * E,), dtype=jnp.float32), 'out_proj_w': jax.random.normal(ks[2], (E, E), dtype=jnp.float32) * s, 'out_proj_b': jnp.zeros((E,), dtype=jnp.float32), 'gate_w': jax.random.normal(ks[3], (NE, E), dtype=jnp.float32) * s, 'gate_b': jnp.zeros((NE,), dtype=jnp.float32), 'expert_w': jax.random.normal(ks[4], (NE, E, E), dtype=jnp.float32) * s, 'expert_b': jnp.zeros((NE, E), dtype=jnp.float32), 'ln1_w': jnp.ones((E,), dtype=jnp.float32), 'ln1_b': jnp.zeros((E,), dtype=jnp.float32), 'ln2_w': jnp.ones((E,), dtype=jnp.float32), 'ln2_b': jnp.zeros((E,), dtype=jnp.float32)}
    _L0_ffn_all = _L0_ffn_setup()
    _L0_ffn_in = {k: v for k, v in _L0_ffn_all.items() if k in ('in_proj_w', 'in_proj_b', 'out_proj_w', 'out_proj_b', 'gate_w', 'gate_b', 'expert_w', 'expert_b', 'ln1_w', 'ln1_b', 'ln2_w', 'ln2_b')}
    del _L0_ffn_all
    return {'x': x, 'ctx_1024': ctx_1024, 'g_xattn': g_xattn, 'g_ffn': g_ffn, 'L0_ffn_in_proj_w': _L0_ffn_in['in_proj_w'], 'L0_ffn_in_proj_b': _L0_ffn_in['in_proj_b'], 'L0_ffn_out_proj_w': _L0_ffn_in['out_proj_w'], 'L0_ffn_out_proj_b': _L0_ffn_in['out_proj_b'], 'L0_ffn_gate_w': _L0_ffn_in['gate_w'], 'L0_ffn_gate_b': _L0_ffn_in['gate_b'], 'L0_ffn_expert_w': _L0_ffn_in['expert_w'], 'L0_ffn_expert_b': _L0_ffn_in['expert_b'], 'L0_ffn_ln1_w': _L0_ffn_in['ln1_w'], 'L0_ffn_ln1_b': _L0_ffn_in['ln1_b'], 'L0_ffn_ln2_w': _L0_ffn_in['ln2_w'], 'L0_ffn_ln2_b': _L0_ffn_in['ln2_b']}

def reference(x, ctx_1024, g_xattn, g_ffn, L0_ffn_in_proj_w, L0_ffn_in_proj_b, L0_ffn_out_proj_w, L0_ffn_out_proj_b, L0_ffn_gate_w, L0_ffn_gate_b, L0_ffn_expert_w, L0_ffn_expert_b, L0_ffn_ln1_w, L0_ffn_ln1_b, L0_ffn_ln2_w, L0_ffn_ln2_b):
    import jax
    import jax.numpy as jnp

    def _L0_xattn_ref(q, k, v):
        import jax, jax.numpy as jnp
        import numpy as np
        NUM_HEADS = 16
        B, S, dim = q.shape
        H = NUM_HEADS
        D = dim // H
        scale = D ** (-0.5)
        qh = q.reshape(B, S, H, D) * scale
        kh = k.reshape(B, S, H, D)
        vh = v.reshape(B, S, H, D)
        scores = jnp.einsum('bqhd,bkhd->bhqk', qh, kh)
        weights = jax.nn.softmax(scores, axis=-1)
        out = jnp.einsum('bhqk,bkhd->bqhd', weights, vh)
        return out.reshape(B, S, dim)

    def _L0_ffn_ref(x, in_proj_w, in_proj_b, out_proj_w, out_proj_b, gate_w, gate_b, expert_w, expert_b, ln1_w, ln1_b, ln2_w, ln2_b):
        import jax, jax.numpy as jnp
        import numpy as np
        NUM_HEADS = 16
        TOP_K = 2
        ROPE_BASE = 10000.0
        LN_EPS = 1e-05

        def _rope_sin_cos(S, D, dtype):
            inv_freq = 1.0 / ROPE_BASE ** (jnp.arange(0, D, 2, dtype=jnp.float32) / D)
            freqs = jnp.arange(S, dtype=jnp.float32)[:, None] * inv_freq[None, :]
            sin = jnp.sin(freqs).astype(dtype)[None, :, None, :]
            cos = jnp.cos(freqs).astype(dtype)[None, :, None, :]
            return (sin, cos)

        def _apply_rope(x, sin, cos):
            x1, x2 = (x[..., 0::2], x[..., 1::2])
            r1 = x1 * cos - x2 * sin
            r2 = x1 * sin + x2 * cos
            return jnp.stack([r1, r2], axis=-1).reshape(x.shape)

        def _layer_norm(x, w, b):
            mu = jnp.mean(x, axis=-1, keepdims=True)
            var = jnp.mean(jnp.square(x - mu), axis=-1, keepdims=True)
            return (x - mu) * jax.lax.rsqrt(var + LN_EPS) * w + b
        B, S, E = x.shape
        H = NUM_HEADS
        D = E // H
        xh = x.reshape(B, S, H, D)
        sin, cos = _rope_sin_cos(S, D, x.dtype)
        q_in = _apply_rope(xh, sin, cos).reshape(B, S, E)
        k_in = q_in
        v_in = x
        Wq, Wk, Wv = jnp.split(in_proj_w, 3, axis=0)
        bq, bk, bv = jnp.split(in_proj_b, 3, axis=0)
        q = (q_in @ Wq.T + bq).reshape(B, S, H, D)
        k = (k_in @ Wk.T + bk).reshape(B, S, H, D)
        v = (v_in @ Wv.T + bv).reshape(B, S, H, D)
        scale = 1.0 / jnp.sqrt(jnp.asarray(D, dtype=x.dtype))
        scores = jnp.einsum('bqhd,bkhd->bhqk', q, k) * scale
        causal = jnp.tril(jnp.ones((S, S), dtype=bool))
        scores = jnp.where(causal[None, None], scores, jnp.asarray(-jnp.inf, dtype=scores.dtype))
        attn = jax.nn.softmax(scores, axis=-1)
        ctx = jnp.einsum('bhqk,bkhd->bqhd', attn, v).reshape(B, S, E)
        attn_out = ctx @ out_proj_w.T + out_proj_b
        x1 = _layer_norm(x + attn_out, ln1_w, ln1_b)
        gates = jax.nn.softmax(x1 @ gate_w.T + gate_b, axis=-1)
        _, top_idx = jax.lax.top_k(gates, TOP_K)
        top_gates = jnp.take_along_axis(gates, top_idx, axis=-1)
        expert_outputs = jnp.einsum('bsd,efd->bsef', x1, expert_w) + expert_b[None, None]
        sel = jnp.take_along_axis(expert_outputs, top_idx[..., None], axis=2)
        moe_out = jnp.sum(sel * top_gates[..., None], axis=2)
        return _layer_norm(x1 + moe_out, ln2_w, ln2_b)
    x = x + jnp.tanh(g_xattn[0]) * _L0_xattn_ref(_layernorm(x, axis=-1), ctx_1024, ctx_1024)
    x = x + jnp.tanh(g_ffn[0]) * _L0_ffn_ref(_layernorm(x, axis=-1), L0_ffn_in_proj_w, L0_ffn_in_proj_b, L0_ffn_out_proj_w, L0_ffn_out_proj_b, L0_ffn_gate_w, L0_ffn_gate_b, L0_ffn_expert_w, L0_ffn_expert_b, L0_ffn_ln1_w, L0_ffn_ln1_b, L0_ffn_ln2_w, L0_ffn_ln2_b)
    return x

_drawn_inputs = setup_inputs


def setup_inputs(seed=0):
    import zlib

    import numpy as np

    out = dict(_drawn_inputs(seed))
    spreads = {'L0_ffn_in_proj_b': (0.0, 0.1),
     'L0_ffn_out_proj_b': (0.0, 0.1),
     'L0_ffn_gate_b': (0.0, 0.1),
     'L0_ffn_expert_b': (0.0, 0.1),
     'L0_ffn_ln1_w': (1.0, 0.2),
     'L0_ffn_ln1_b': (0.0, 0.1),
     'L0_ffn_ln2_w': (1.0, 0.2),
     'L0_ffn_ln2_b': (0.0, 0.1)}
    factors = {}
    for name, (base, spread) in spreads.items():
        noise = np.random.default_rng([zlib.crc32(name.encode()), seed]).standard_normal(out[name].shape)
        drawn = base * np.exp(spread * noise) if base else spread * noise
        out[name] = jnp.asarray(drawn.astype(out[name].dtype))
    for name, factor in factors.items():
        out[name] = (out[name] * factor).astype(out[name].dtype)
    return out
```

```python
from contextlib import ExitStack

import numpy as np

import concourse.bass as bass
from concourse import mybir

ALU = mybir.AluOpType
ACT = mybir.ActivationFunctionType
AX_X = mybir.AxisListType.X
F32 = mybir.dt.float32
BF16 = mybir.dt.bfloat16

P = 128
B = 32
H = 16
D = P // H
NE = 8
G = 2
GROUPS = B // G
TILES = G * 4
HEADS = 4
RING = 3
PROWS = 64
SROWS = 6 * D
MROWS = SROWS + 3
SLOT_Q = {0: 0, 1: 0, 2: 0, 3: 1, 4: 1, 5: 2}
SLOT_K = {0: 0, 1: 1, 2: 2, 3: 0, 4: 1, 5: 0}
STACK_DMAS = 2 * 2 * 6
SCALE = float(D) ** -0.5
EPS = 1e-5
MASKED = -1e30
LAST = GROUPS - 1
TILE_PA = [(0, 0), (1, 0), (0, 1), (1, 1)]


def gated_block_kernel(nc, x, ctx_in, g_x, g_f, wq_t, wk_t, wv_t, wo_t, bq, bk, bv, bo,
                       gate_t, gate_b, exp_t, exp_b, ln1w, ln1b, ln2w, ln2b,
                       cos_t, sin_t, ident, identb, mask_qk, mask_kq, out):
    es = ExitStack()
    with es:
        def sb(name, shape, dt=F32):
            return es.enter_context(nc.sbuf_tensor(name, shape, dt))

        def sem(name):
            return es.enter_context(nc.semaphore(name))

        def tok(t):
            return t.rearrange("b s d -> s b d")

        x2_dram = nc.dram_tensor("x2_scratch", [B, P, P], F32, kind="Internal").ap()
        xn2_dram = nc.dram_tensor("xn2_scratch", [B, P, P], F32, kind="Internal").ap()
        att_dram = nc.dram_tensor("att_scratch", [B, P, P], F32, kind="Internal").ap()

        idf = sb("idf", [P, P])
        idb = sb("idb", [P, P], BF16)
        mqk = sb("mqk", [P, P], BF16)
        mkq = sb("mkq", [P, P], BF16)
        wq = sb("wq", [P, P]); wk = sb("wk", [P, P]); wv = sb("wv", [P, P]); wo = sb("wo", [P, P])
        bqs = sb("bqs", [P, 1]); bks = sb("bks", [P, 1]); bqsc = sb("bqsc", [P, 1])
        bvb = sb("bvb", [P, P]); bob = sb("bob", [P, P])
        gwt = sb("gwt", [P, NE]); gbb = sb("gbb", [P, NE])
        ewt = sb("ewt", [P, NE * P]); ebs = sb("ebs", [NE, P])
        l1w = sb("l1w", [P, P]); l1b = sb("l1b", [P, P]); l2w = sb("l2w", [P, P]); l2b = sb("l2b", [P, P])
        cost = sb("cost", [P, P]); sint = sb("sint", [P, P])
        gates = sb("gates_in", [P, 2]); tg = sb("tg", [P, 2])
        mhalf = sb("mhalf", [P, G])
        qst = [sb(f"qst{i}", [P, 8, G * P], BF16) for i in range(RING)]
        kst = [sb(f"kst{i}", [P, 8, G * P], BF16) for i in range(RING)]
        vaug = [sb(f"vaug{i}", [P, G, H, D + 1]) for i in range(RING)]
        xa = [sb(f"xa{i}", [P, G, P]) for i in range(RING)]
        ca = [sb(f"ca{i}", [P, G, P]) for i in range(RING)]
        xb = [sb(f"xb{i}", [P, P]) for i in range(G)]
        stats = sb("stats", [P, G, 6]); mv = sb("mv", [P, G, 2]); ve = sb("ve", [P, G]); rstd = sb("rstd", [P, G])
        xp = sb("xp", [P, G, P]); cp = sb("cp", [P, G, P])
        xn2 = sb("xn2", [P, G, P]); rc = sb("rc", [P, G, P]); rs = sb("rs", [P, G, P]); xr = sb("xr", [P, G, P])
        txr = sb("txr", [P, 2 * G * P])
        t32 = sb("t32", [P, 2 * G * P]); r32 = sb("r32", [P, 2 * G * P])
        part = [sb(f"part{i}", [P, 2 * G * P], BF16) for i in range(3)]
        nm = [sb(f"nm{i}", [P, H]) for i in range(G)]
        mr = [sb(f"mr{i}", [P, H]) for i in range(G)]
        mst = [sb(f"mst{i}", [P, 2, 3, 8], BF16) for i in range(G)]
        mts = [sb(f"mts{i}", [48, P], BF16) for i in range(G)]
        pt = [sb(f"pt{i}", [P, HEADS, P]) for i in range(4)]
        us = sb("us", [P, 4, P])
        rec = sb("rec", [P, H]); ao = [sb(f"ao{i}", [P, P]) for i in range(G)]
        xo = [sb(f"xo{i}", [P, P]) for i in range(G)]

        def ps(name, shape, dt=F32):
            return es.enter_context(nc.psum_tensor(name, shape, dt))
        s_bank = [ps(f"s_bank{i}", [P, 512]) for i in range(2)]
        st_bank = [ps(f"st_bank{i}", [P, 512]) for i in range(2)]
        u_bank = ps("u_bank", [P, 512])
        t_bank = ps("t_bank", [P, 512])
        n_bank = ps("n_bank", [P, 512])
        m_bank = ps("m_bank", [P, 512])
        m_bank_b = m_bank[:, :].bitcast(BF16)

        c_dma = sem("constants_loaded"); c_set = sem("constants_set"); c_tanh = sem("tanh_ready"); c_low = sem("lower_set")
        sp_mark = sem("sp_waits_end"); pool_mark = sem("pool_waits_end"); dve_mark = sem("dve_waits_end"); pe_mark = sem("pe_waits_end")
        NCONST = 24

        class Sems:
            pass

        def sems(ph):
            s = Sems()
            s.xa_in = sem(ph + "_input_loaded")
            s.xb_in = [sem(f"{ph}_residual_loaded{b}") for b in range(G)]
            s.stat = sem(ph + "_stats"); s.ln = sem(ph + "_ln_steps"); s.v = sem(ph + "_v_ready")
            s.perm = sem(ph + "_context_permuted")
            s.tr = sem(ph + "_transposed"); s.txr = sem(ph + "_inputs_t_copied")
            s.proj = sem(ph + "_qk_projected"); s.vproj = sem(ph + "_v_projected")
            s.t32 = sem(ph + "_qk_t_copied"); s.split = sem(ph + "_split_steps")
            s.stack = sem(ph + "_stacks_written")
            s.s = sem(ph + "_scores"); s.max = sem(ph + "_max")
            s.msplit = sem(ph + "_max_split_steps"); s.mt = sem(ph + "_max_transposed")
            s.mts = sem(ph + "_max_t_copied"); s.mdma = [sem(f"{ph}_max_rows_written{b}") for b in range(G)]
            s.st = sem(ph + "_scores_t"); s.exp = sem(ph + "_exp"); s.av = sem(ph + "_av")
            s.ucopy = sem(ph + "_u_copied"); s.ut = sem(ph + "_u_transposed")
            s.rec = sem(ph + "_reciprocal"); s.norm = sem(ph + "_normalised")
            s.res = sem(ph + "_residual_added")
            s.stored = [sem(f"{ph}_stored{b}") for b in range(G)]
            s.xnst = sem(ph + "_xn2_stored")
            return s

        SX, SY = sems("x"), sems("y")

        LOOP_START = 4
        LOOP_END = LOOP_START + (GROUPS - 2 - LOOP_START) // RING * RING

        def steps(eng, body):
            for s in range(-1, LOOP_START):
                body(s, s)
            with eng.Fori(LOOP_START, LOOP_END - RING + 1, RING) as i:
                for k in range(RING):
                    body(i + k, LOOP_START + k)
            for s in range(LOOP_END, GROUPS + 3):
                body(s, s)

        def has(sc, lag):
            return 0 <= sc - lag < GROUPS

        def at_least(eng, semaphore, value, real):
            if real > 0:
                eng.wait_ge(semaphore, value)

        def waits_end(eng, mark):
            eng.sem_inc(mark, 1)

        def sp_phase(sp, S, masked):
            src = x2_dram if masked else x

            def load(g, gc):
                if gc >= 1:
                    sp.wait_ge(S.xa_in, g * (16 if masked else 32))
                    waits_end(sp, sp_mark)
                if gc >= RING:
                    at_least(sp, S.tr, g - RING + 1, gc - RING + 1)
                    if not masked:
                        sp.wait_ge(S.v, g - RING + 1)
                waits_end(sp, sp_mark)
                sp.dma_start(xa[gc % RING][:, :, :], tok(src)[:, bass.ds(g * G, G), :]).then_inc(S.xa_in, 16)
                if not masked:
                    sp.dma_start(ca[gc % RING][:, :, :], tok(ctx_in)[:, bass.ds(g * G, G), :]).then_inc(S.xa_in, 16)

            def stacks(g, gc):
                if gc >= RING:
                    sp.wait_ge(S.st, (g - RING + 1) * TILES)
                for p_i, need in ((0, 1), (1, 3), (2, 4)):
                    sp.wait_ge(S.split, g * 4 + need)
                    for dst, slots, off in ((qst, SLOT_Q, 0), (kst, SLOT_K, G * P)):
                        for slot in range(6):
                            if slots[slot] != p_i:
                                continue
                            for p in range(2):
                                r = PROWS * p + D * slot
                                sp.dma_start(dst[gc % RING][r:r + D, :, :],
                                             part[p_i][PROWS * p:PROWS * (p + 1), off:off + G * P]
                                             ).then_inc(S.stack, 16)

            def max_rows(g, gc, b):
                sp.wait_ge(S.mts, g * G + b + 1)
                for p in range(2):
                    r = PROWS * p + SROWS
                    sp.dma_start(qst[gc % RING][r:r + 3, :, b * P:(b + 1) * P],
                                 mts[b][24 * p:24 * p + 24, :]).then_inc(S.mdma[b], 16)

            def residual(g, gc, b):
                if gc >= 1:
                    sp.wait_ge(S.res, (g - 1) * G + b + 1)
                waits_end(sp, sp_mark)
                sp.dma_start(xb[b][:, :], tok(x)[:, bass.ds(g * G + b, 1), :].rearrange("s o d -> s (o d)")
                             ).then_inc(S.xb_in[b], 16)

            def store(g, gc, b):
                if masked:
                    sp.wait_ge(S.norm, g * G + b + 1)
                    waits_end(sp, sp_mark)
                    sp.dma_start(tok(att_dram)[:, bass.ds(g * G + b, 1), :].rearrange("s o d -> s (o d)"),
                                 ao[b][:, :]).then_inc(S.stored[b], 16)
                else:
                    sp.wait_ge(S.res, g * G + b + 1)
                    waits_end(sp, sp_mark)
                    sp.dma_start(tok(x2_dram)[:, bass.ds(g * G + b, 1), :].rearrange("s o d -> s (o d)"),
                                 xo[b][:, :]).then_inc(S.stored[b], 16)

            def body(s, c):
                if has(c, -1):
                    if c == -1:
                        load(0, 0)
                if has(c, -2):
                    load(s + 2, c + 2)
                if has(c, 3):
                    store(s - 3, c - 3, 1)
                if has(c, 2):
                    max_rows(s - 2, c - 2, 1)
                    if not masked:
                        residual(s - 2, c - 2, 0)
                if masked and has(c, -1):
                    sp.wait_ge(S.ln, (s + 2) * LN_STEPS_Y)
                    waits_end(sp, sp_mark)
                    sp.dma_start(tok(xn2_dram)[:, bass.ds((s + 1) * G, G), :], xn2[:, :, :]).then_inc(S.xnst, 16)
                if has(c, 0):
                    stacks(s, c)
                if has(c, 1):
                    max_rows(s - 1, c - 1, 0)
                if has(c, 2):
                    if not masked:
                        residual(s - 2, c - 2, 1)
                    store(s - 2, c - 2, 0)
            if masked:
                for b in range(G):
                    sp.wait_ge(SX.stored[b], 16 * GROUPS)
            steps(sp, body)

        LN_STEPS_X = 4
        LN_STEPS_Y = 8

        def pool_phase(pool, S, masked):
            def ln(g, gc):
                n = LN_STEPS_Y if masked else LN_STEPS_X
                k = g * n
                buf = xa[gc % RING]
                pool.wait_ge(S.stat, (g + 1) * 4)
                waits_end(pool, pool_mark)
                pool.tensor_scalar(ve[:, :], mv[:, :, 1], EPS, None, ALU.add).then_inc(S.ln, 1)
                pool.wait_ge(S.ln, k + 1)
                pool.tensor_tensor(rstd[:, :], ve[:, :], mhalf[:, :], ALU.pow).then_inc(S.ln, 1)
                pool.wait_ge(S.ln, k + 2)
                if not masked:
                    if gc >= 1:
                        pool.wait_ge(S.tr, g)
                    waits_end(pool, pool_mark)
                    for b in range(G):
                        pool.tensor_scalar(xp[:, b, :].rearrange("q (p d c) -> q p c d", p=2, d=D),
                                           buf[:, b, :].rearrange("q (p c d) -> q p c d", p=2, d=D),
                                           mv[:, b, 0:1], rstd[:, b:b + 1], ALU.subtract, ALU.mult).then_inc(S.ln, 1)
                    return
                if gc >= 1:
                    pool.wait_ge(S.tr, g)
                    pool.wait_ge(S.xnst, g * 16)
                waits_end(pool, pool_mark)
                for b in range(G):
                    pool.tensor_scalar(xn2[:, b, :], buf[:, b, :], mv[:, b, 0:1], rstd[:, b:b + 1],
                                       ALU.subtract, ALU.mult).then_inc(S.ln, 1)
                pool.wait_ge(S.ln, k + 4)
                pairs = xn2[:, :, :].rearrange("q b (i e) -> q b i e", e=2)
                rot = rs[:, :, :].rearrange("q b (i e) -> q b i e", e=2)
                sg = sint[:, :].rearrange("q (i e) -> q i e", e=2)
                pool.tensor_tensor(rc[:, :, :], xn2[:, :, :], cost[:, :].unsqueeze(1).broadcast_to([P, G, P]),
                                   ALU.mult).then_inc(S.ln, 1)
                for e in range(2):
                    pool.tensor_tensor(rot[:, :, :, e], pairs[:, :, :, 1 - e],
                                       sg[:, :, e].unsqueeze(1).broadcast_to([P, G, P // 2]),
                                       ALU.mult).then_inc(S.ln, 1)
                pool.wait_ge(S.ln, k + 7)
                pool.tensor_tensor(xr[:, :, :], rc[:, :, :], rs[:, :, :], ALU.add).then_inc(S.ln, 1)

            def values(g, gc):
                if gc >= RING:
                    pool.wait_ge(S.av, (g - RING + 1) * TILES)
                pool.wait_ge(S.xa_in, (g + 1) * 32)
                waits_end(pool, pool_mark)
                pool.tensor_scalar(vaug[gc % RING][:, :, :, 0:D].rearrange("k b h d -> k (b h) d"),
                                   ca[gc % RING][:, :, :].rearrange("k b (h d) -> k (b h) d", d=D),
                                   0.0, None, ALU.add).then_inc(S.v, 1)

            def split(g, gc):
                k = g * 4
                pool.wait_ge(S.t32, (g + 1) * 2)
                if gc >= 1:
                    pool.wait_ge(S.stack, g * STACK_DMAS * 16)
                waits_end(pool, pool_mark)
                pool.tensor_scalar(part[0][:, :], t32[:, :], 0.0, None, ALU.add).then_inc(S.split, 1)
                pool.wait_ge(S.split, k + 1)
                pool.tensor_tensor(r32[:, :], t32[:, :], part[0][:, :], ALU.subtract).then_inc(S.split, 1)
                pool.wait_ge(S.split, k + 2)
                waits_end(pool, pool_mark)
                pool.tensor_scalar(part[1][:, :], r32[:, :], 0.0, None, ALU.add).then_inc(S.split, 1)
                pool.wait_ge(S.split, k + 3)
                pool.tensor_tensor(part[2][:, :], r32[:, :], part[1][:, :], ALU.subtract).then_inc(S.split, 1)

            def max_split(g, gc, b):
                k = (g * G + b) * 4
                half = nm[b][:, :].rearrange("q (p c) -> q p c", p=2)
                rest = mr[b][:, :].rearrange("q (p c) -> q p c", p=2)
                pool.wait_ge(S.max, g * TILES + 4 * b + 4)
                if gc >= 1:
                    pool.wait_ge(S.mt, (g - 1) * G + b + 1)
                waits_end(pool, pool_mark)
                pool.tensor_scalar(mst[b][:, :, 0, :], half, 0.0, None, ALU.add).then_inc(S.msplit, 1)
                pool.wait_ge(S.msplit, k + 1)
                pool.tensor_tensor(rest, half, mst[b][:, :, 0, :], ALU.subtract).then_inc(S.msplit, 1)
                pool.wait_ge(S.msplit, k + 2)
                waits_end(pool, pool_mark)
                pool.tensor_scalar(mst[b][:, :, 1, :], rest, 0.0, None, ALU.add).then_inc(S.msplit, 1)
                pool.wait_ge(S.msplit, k + 3)
                pool.tensor_tensor(mst[b][:, :, 2, :], rest, mst[b][:, :, 1, :], ALU.subtract).then_inc(S.msplit, 1)

            def add_residual(g, gc, b):
                pool.wait_ge(S.norm, g * G + b + 1)
                pool.wait_ge(S.xb_in[b], (g + 1) * 16)
                if gc >= 1:
                    pool.wait_ge(S.stored[b], g * 16)
                pool.tensor_tensor(xo[b][:, :], xb[b][:, :], ao[b][:, :], ALU.add).then_inc(S.res, 1)

            def body(s, c):
                if has(c, 2):
                    max_split(s - 2, c - 2, 1)
                if has(c, 3) and not masked:
                    add_residual(s - 3, c - 3, 1)
                if has(c, 0):
                    if not masked:
                        values(s, c)
                    split(s, c)
                if has(c, 1):
                    max_split(s - 1, c - 1, 0)
                if has(c, -1):
                    ln(s + 1, c + 1)
                if has(c, 2) and not masked:
                    add_residual(s - 2, c - 2, 0)
            steps(pool, body)

        def pe_phase(pe, S, masked):
            def tr(g, gc):
                if gc >= 1:
                    pe.wait_ge(S.t32, g * 2)
                if masked:
                    pe.wait_ge(S.ln, (g + 1) * LN_STEPS_Y)
                    srcs = [xr[:, 0, :], xr[:, 1, :], xn2[:, 0, :], xn2[:, 1, :]]
                else:
                    pe.wait_ge(S.ln, (g + 1) * LN_STEPS_X)
                    pe.wait_ge(S.perm, (g + 1) * G)
                    srcs = [xp[:, 0, :], xp[:, 1, :], cp[:, 0, :], cp[:, 1, :]]
                for i, a in enumerate(srcs):
                    ins = pe.transpose(t_bank[:, i * P:(i + 1) * P], a, idf[:, :])
                ins.then_inc(S.tr, 1)

            def project(g, gc):
                pe.wait_ge(S.txr, g + 1)
                pe.matmul(t_bank[:, 0:G * P], wq[:, :], txr[:, 0:G * P], start=True, stop=True)
                pe.matmul(t_bank[:, G * P:2 * G * P], wk[:, :], txr[:, 0:G * P],
                          start=True, stop=True).then_inc(S.proj, 1)

            def project_v(g, gc):
                if gc >= 2:
                    pe.wait_ge(S.mts, (g - 1) * G)
                for b in range(G):
                    ins = pe.matmul(m_bank[:, b * P:(b + 1) * P], txr[:, (G + b) * P:(G + b + 1) * P], wv[:, :],
                                    start=True, stop=True)
                ins.then_inc(S.vproj, 1)

            def scores(g, gc, t):
                b, (p, a) = t // 4, TILE_PA[t % 4]
                bank = s_bank[t % 2]
                if t == 0:
                    pe.wait_ge(S.stack, (g + 1) * STACK_DMAS * 16)
                if gc >= 1 or t >= 2:
                    pe.wait_ge(S.max, g * TILES + t - 1)
                if masked:
                    pe.matmul(bank[:, :], idb[:, :], mqk[:, :].unsqueeze(1).broadcast_to([P, HEADS, P]),
                              start=True, stop=False, skip_group_check=True)
                r = PROWS * p
                for j in range(HEADS):
                    ins = pe.matmul(bank[:, j * P:(j + 1) * P],
                                    qst[gc % RING][r:r + SROWS, 4 * a + j, b * P:(b + 1) * P],
                                    kst[gc % RING][r:r + SROWS, 4 * a + j, b * P:(b + 1) * P],
                                    start=not masked, stop=True, skip_group_check=masked)
                ins.then_inc(S.s, 1)

            def scores_t(g, gc, t):
                b, (p, a) = t // 4, TILE_PA[t % 4]
                bank = st_bank[t % 2]
                if t % 4 == 0:
                    pe.wait_ge(S.mdma[b], (g + 1) * 32)
                if gc >= 1 or t >= 2:
                    pe.wait_ge(S.exp, g * TILES + t - 1)
                if masked:
                    pe.matmul(bank[:, :], idb[:, :], mkq[:, :].unsqueeze(1).broadcast_to([P, HEADS, P]),
                              start=True, stop=False, skip_group_check=True)
                r = PROWS * p
                for j in range(HEADS):
                    ins = pe.matmul(bank[:, j * P:(j + 1) * P],
                                    kst[gc % RING][r:r + MROWS, 4 * a + j, b * P:(b + 1) * P],
                                    qst[gc % RING][r:r + MROWS, 4 * a + j, b * P:(b + 1) * P],
                                    start=not masked, stop=True, skip_group_check=masked)
                ins.then_inc(S.st, 1)

            def av(g, gc, t):
                b, (p, a) = t // 4, TILE_PA[t % 4]
                pe.wait_ge(S.exp, g * TILES + t + 1)
                if t == 0:
                    pe.wait_ge(S.v, g + 1)
                if t % 4 == 0 and (gc >= 1 or b):
                    pe.wait_ge(S.ucopy, g * G + b)
                r = 2 * p + a
                for j in range(HEADS):
                    ins = pe.matmul(u_bank[32 * j:32 * j + D + 1, r * P:(r + 1) * P],
                                    vaug[gc % RING][:, b, 4 * r + j, :], pt[t % 4][:, j, :],
                                    start=True, stop=True)
                ins.then_inc(S.av, 1)

            def transpose_max(g, gc, b):
                pe.wait_ge(S.msplit, (g * G + b + 1) * 4)
                if masked:
                    if b == 1 or gc >= 1:
                        at_least(pe, S.mts, g * G + b, gc * G + b)
                    if gc + 1 < GROUPS:
                        pe.wait_ge(S.v, g + 2)
                elif gc >= 1 or b:
                    pe.wait_ge(S.mts, g * G + b)
                waits_end(pe, pe_mark)
                pe.transpose(m_bank_b[0:48, 0:P], mst[b][:, :, :, :].rearrange("q p r c -> q (p r c)"), idb[:, :]).then_inc(S.mt, 1)

            def transpose_u(g, gc, b):
                pe.wait_ge(S.ucopy, g * G + b + 1)
                if gc >= 1 or b:
                    pe.wait_ge(S.norm, g * G + b)
                for r in range(4):
                    ins = pe.transpose(n_bank[:, r * P:(r + 1) * P], us[:, r, :], idf[:, :])
                ins.then_inc(S.ut, 1)

            def body(s, c):
                if has(c, 0):
                    tr(s, c)
                for t in range(TILES):
                    if has(c, 1):
                        scores(s - 1, c - 1, t)
                    if t == 0 and has(c, 0) and masked:
                        project(s, c)
                    if t == 2 and has(c, 0) and masked:
                        project_v(s, c)
                    if has(c, 2):
                        scores_t(s - 2, c - 2, t)
                        if t >= 1:
                            av(s - 2, c - 2, t - 1)
                    if t == 1:
                        if has(c, 2):
                            transpose_max(s - 2, c - 2, 1)
                        if has(c, 3):
                            transpose_u(s - 3, c - 3, 1)
                    if t == 5:
                        if has(c, 1):
                            transpose_max(s - 1, c - 1, 0)
                        if has(c, 2):
                            transpose_u(s - 2, c - 2, 0)
                if has(c, 2):
                    av(s - 2, c - 2, TILES - 1)
            steps(pe, body)

        def act_phase(act, S, masked):
            def copy_t(g, gc):
                if gc >= 1 and not masked:
                    act.wait_ge(S.split, g * 4)
                act.wait_ge(S.tr, g + 1)
                if masked:
                    if gc >= 1:
                        act.wait_ge(S.vproj, g)
                    act.activation(txr[:, :], t_bank[:, :], ACT.Copy).then_inc(S.txr, 1)
                    return
                act.activation(t32[:, 0:G * P], t_bank[:, 0:G * P], ACT.Copy, scale=SCALE).then_inc(S.t32, 1)
                act.activation(t32[:, G * P:], t_bank[:, G * P:], ACT.Copy).then_inc(S.t32, 1)

            def copy_qk(g, gc):
                if gc >= 1:
                    act.wait_ge(S.split, g * 4)
                act.wait_ge(S.proj, g + 1)
                act.activation(t32[:, 0:G * P], t_bank[:, 0:G * P], ACT.Identity, bias=bqsc[:, :],
                               scale=SCALE).then_inc(S.t32, 1)
                act.activation(t32[:, G * P:], t_bank[:, G * P:], ACT.Identity, bias=bks[:, :]).then_inc(S.t32, 1)

            def exp(g, gc, t):
                act.wait_ge(S.st, g * TILES + t + 1)
                if gc >= 1 or t >= 4:
                    act.wait_ge(S.av, g * TILES + t - 3)
                act.activation(pt[t % 4][:, :, :].rearrange("k j q -> k (j q)"), st_bank[t % 2][:, :],
                               ACT.Exp).then_inc(S.exp, 1)

            def copy_max(g, gc, b):
                act.wait_ge(S.mt, g * G + b + 1)
                if gc >= 1:
                    act.wait_ge(S.mdma[b], g * 32)
                act.activation(mts[b][:, :], m_bank_b[0:48, 0:P], ACT.Copy).then_inc(S.mts, 1)

            def copy_u(g, gc, b):
                act.wait_ge(S.av, g * TILES + 4 * b + 4)
                if gc >= 1 or b:
                    act.wait_ge(S.ut, g * G + b)
                act.activation(us[:, :, :].rearrange("p r q -> p (r q)"), u_bank[:, :], ACT.Copy).then_inc(S.ucopy, 1)

            def body(s, c):
                if has(c, 3):
                    copy_u(s - 3, c - 3, 1)
                if has(c, 0):
                    copy_t(s, c)
                for t in range(TILES):
                    if has(c, 2):
                        exp(s - 2, c - 2, t)
                    if t == 1 and has(c, 0) and masked:
                        copy_qk(s, c)
                    if t == 1 and has(c, 2):
                        copy_max(s - 2, c - 2, 1)
                    if t == 4 and has(c, 2):
                        copy_u(s - 2, c - 2, 0)
                    if t == 5 and has(c, 1):
                        copy_max(s - 1, c - 1, 0)
            steps(act, body)

        def dve_phase(dve, S, masked):
            def stat(g, gc):
                dve.wait_ge(S.xa_in, (g + 1) * (16 if masked else 32))
                if gc >= 1:
                    dve.wait_ge(S.ln, g * (LN_STEPS_Y if masked else LN_STEPS_X))
                for b in range(G):
                    dve.bn_stats(stats[:, b, :], xa[gc % RING][:, b, :]).then_inc(S.stat, 1)
                if not masked:
                    if gc >= 1:
                        dve.wait_ge(S.tr, g)
                    for b in range(G):
                        dve.tensor_copy(cp[:, b, :].rearrange("k (p d c) -> k p c d", p=2, d=D),
                                        ca[gc % RING][:, b, :].rearrange("k (p c d) -> k p c d", p=2, d=D)
                                        ).then_inc(S.perm, 1)
                dve.wait_ge(S.stat, g * 4 + 2)
                waits_end(dve, dve_mark)
                for b in range(G):
                    dve.bn_aggr(mv[:, b, :], stats[:, b, :]).then_inc(S.stat, 1)

            def values(g, gc):
                dve.wait_ge(S.vproj, g + 1)
                if gc >= RING:
                    dve.wait_ge(S.av, (g - RING + 1) * TILES)
                dve.tensor_tensor(vaug[gc % RING][:, :, :, 0:D],
                                  m_bank[:, 0:G * P].rearrange("k (b h d) -> k b h d", b=G, d=D),
                                  bvb[:, :].rearrange("k (h d) -> k h d", d=D).unsqueeze(1)
                                  .broadcast_to([P, G, H, D]), ALU.add).then_inc(S.v, 1)

            def maxima(g, gc, t):
                b, (p, a) = t // 4, TILE_PA[t % 4]
                dve.wait_ge(S.s, g * TILES + t + 1)
                if gc >= 1 and t % 4 == 0:
                    dve.wait_ge(S.msplit, ((g - 1) * G + b + 1) * 4)
                dve.tensor_reduce(nm[b][:, 8 * p + 4 * a:8 * p + 4 * a + 4],
                                  s_bank[t % 2][:, :].rearrange("q (j k) -> q j k", j=HEADS),
                                  AX_X, ALU.max, negate=True).then_inc(S.max, 1)

            def normalise(g, gc, b):
                view = n_bank[:, :].rearrange("q (h w) -> q h w", w=32)
                dve.wait_ge(S.ut, g * G + b + 1)
                dve.reciprocal(rec[:, :], view[:, :, D]).then_inc(S.rec, 1)
                dve.wait_ge(S.rec, g * G + b + 1)
                o = ao[b][:, :].rearrange("q (h d) -> q h d", d=D)
                rb = rec[:, :].unsqueeze(2).broadcast_to([P, H, D])
                if masked:
                    if gc >= 1:
                        dve.wait_ge(S.stored[b], g * 16)
                    dve.tensor_tensor(o, view[:, :, 0:D], rb, ALU.mult).then_inc(S.norm, 1)
                else:
                    if gc >= 1:
                        dve.wait_ge(S.res, (g - 1) * G + b + 1)
                    dve.scalar_tensor_tensor(out=o, in0=view[:, :, 0:D], scalar=tg[:, 0:1], in1=rb,
                                             op0=ALU.mult, op1=ALU.mult).then_inc(S.norm, 1)

            def body(s, c):
                for t in range(TILES):
                    if has(c, 1):
                        maxima(s - 1, c - 1, t)
                    if t == 1 and has(c, 3):
                        normalise(s - 3, c - 3, 1)
                    if t == 2 and has(c, 0) and masked:
                        values(s, c)
                    if t == 3 and has(c, -1):
                        stat(s + 1, c + 1)
                    if t == 5 and has(c, 2):
                        normalise(s - 2, c - 2, 0)
            steps(dve, body)

        zx2 = [sb(f"zx2_{i}", [P, P]) for i in range(2)]
        zxn = [sb(f"zxn_{i}", [P, P]) for i in range(2)]
        zat = [sb(f"zat_{i}", [P, P]) for i in range(2)]
        zxb = [sb(f"zxb_{i}", [P, P]) for i in range(2)]
        zot = [sb(f"zot_{i}", [P, P]) for i in range(2)]
        zh = [sb(f"zh_{i}", [P, P]) for i in range(2)]
        zmv = [sb(f"zmv_{i}", [P, 8]) for i in range(2)]
        zvr = [sb(f"zvr_{i}", [P, 2]) for i in range(2)]
        zn = [sb(f"zn_{i}", [P, P]) for i in range(2)]
        zx1 = [sb(f"zx1_{i}", [P, P]) for i in range(2)]
        zx1t = [sb(f"zx1t_{i}", [P, P]) for i in range(2)]
        zl = [sb(f"zl_{i}", [P, NE]) for i in range(2)]
        zm = [sb(f"zm_{i}", [P, 1]) for i in range(2)]
        zp = [sb(f"zp_{i}", [P, NE]) for i in range(2)]
        zs = [sb(f"zs_{i}", [P, 2]) for i in range(2)]
        zc = [sb(f"zc_{i}", [P, NE, NE]) for i in range(2)]
        zd = [sb(f"zd_{i}", [P, NE, NE]) for i in range(2)]
        zk = [sb(f"zk_{i}", [P, NE]) for i in range(2)]
        zg = [sb(f"zg_{i}", [P, NE]) for i in range(2)]
        zgt = [sb(f"zgt_{i}", [NE, P]) for i in range(2)]
        zacc = [[sb(f"zacc_{i}_{j}", [P, P]) for j in range(2)] for i in range(2)]
        zy = [sb(f"zy_{i}", [P, P]) for i in range(2)]
        zo = [sb(f"zo_{i}", [P, P]) for i in range(2)]
        lower = sb("lower", [P, NE, NE])

        z_in = sem("z_inputs_loaded"); z_xb = sem("z_bias_added"); z_ot = sem("z_att_transposed")
        z_otc = sem("z_att_t_copied"); z_proj = sem("z_projected"); z_h = sem("z_ln1_steps")
        z_rs = sem("z_rstd_steps"); z_x1 = sem("z_x1_steps"); z_x1t = sem("z_x1_transposed")
        z_x1c = sem("z_x1_t_copied"); z_lg = sem("z_logits"); z_gate = sem("z_gate_steps")
        z_exp = sem("z_gate_exp"); z_gt = sem("z_gates_transposed"); z_gtc = sem("z_gates_t_copied")
        z_y = sem("z_experts"); z_yb = sem("z_expert_bias"); z_acc = sem("z_accumulated")
        z_rs2 = sem("z_rstd2_steps"); z_fin = sem("z_final_steps"); z_out = sem("z_stored")
        ACC = 11
        H1 = 3
        GATE = 7
        FIN = 5

        def pairs_of_steps(eng, body, lag):
            for s in range(0, 4):
                body(s, s)
            with eng.Fori(4, B - 1, 2) as i:
                body(i, 4)
                body(i + 1, 5)
            for s in range(B, B + lag):
                body(s, s)

        def in_z(c, lag):
            return 0 <= c - lag < B

        def seq(t, g):
            return tok(t)[:, bass.ds(g, 1), :].rearrange("s o d -> s (o d)")

        def z_sp(sp):
            for b in range(G):
                sp.wait_ge(SY.stored[b], 16 * GROUPS)
            sp.wait_ge(SY.xnst, 16 * GROUPS)

            def load(g, gc):
                i = gc % 2
                if gc >= 1:
                    sp.wait_ge(z_in, g * 48)
                    waits_end(sp, sp_mark)
                if gc >= 2:
                    sp.wait_ge(z_fin, (g - 1) * FIN)
                waits_end(sp, sp_mark)
                sp.dma_start(zx2[i][:, :], seq(x2_dram, g)).then_inc(z_in, 16)
                sp.dma_start(zxn[i][:, :], seq(xn2_dram, g)).then_inc(z_in, 16)
                sp.dma_start(zat[i][:, :], seq(att_dram, g)).then_inc(z_in, 16)

            def body(s, c):
                if in_z(c, 0):
                    load(s, c)
                if in_z(c, 2):
                    sp.wait_ge(z_fin, (s - 1) * FIN)
                    waits_end(sp, sp_mark)
                    if c > 2:
                        sp.wait_ge(z_out, (s - 2) * 16)
                    waits_end(sp, sp_mark)
                    sp.dma_start(seq(out, s - 2), zo[c % 2][:, :]).then_inc(z_out, 16)
            pairs_of_steps(sp, body, 2)
            sp.wait_ge(z_out, 16 * B)

        def z_pe(pe):
            def front(g, gc):
                i = gc % 2
                pe.wait_ge(z_in, (g + 1) * 48)
                if gc >= 1:
                    pe.wait_ge(z_otc, g)
                pe.transpose(t_bank[:, 0:P], zat[i][:, :], idf[:, :]).then_inc(z_ot, 1)
                pe.wait_ge(z_otc, g + 1)
                if gc >= 1:
                    pe.wait_ge(z_h, (g - 1) * H1 + 1)
                pe.matmul(m_bank[:, 0:P], zot[i][:, :], wo[:, :], start=True, stop=True).then_inc(z_proj, 1)

            def back(g, gc):
                i = gc % 2
                pe.wait_ge(z_x1, (g + 1) * 3)
                if gc >= 1:
                    pe.wait_ge(z_gtc, g)
                pe.transpose(n_bank[:, 0:P], zx1[i][:, :], idf[:, :]).then_inc(z_x1t, 1)
                pe.wait_ge(z_x1c, g + 1)
                pe.matmul(n_bank[:, 0:NE], zx1t[i][:, :], gwt[:, :], start=True, stop=True).then_inc(z_lg, 1)
                for k in range(2):
                    bank = (s_bank if gc % 2 == 0 else st_bank)[k]
                    if gc >= 2:
                        pe.wait_ge(z_acc, (g - 1) * ACC)
                    ins = pe.matmul(bank[:, :], zx1t[i][:, :], ewt[:, k * 512:(k + 1) * 512], start=True, stop=True)
                ins.then_inc(z_y, 1)
                pe.wait_ge(z_gate, (g + 1) * GATE)
                pe.transpose(n_bank[0:NE, 0:P], zg[i][:, :], idf[:, :]).then_inc(z_gt, 1)
                pe.wait_ge(z_gtc, g + 1)
                if gc >= 1:
                    pe.wait_ge(z_acc, (g - 1) * ACC + 1)
                pe.matmul(u_bank[:, 0:P], zgt[i][:, :], ebs[:, :], start=True, stop=True).then_inc(z_yb, 1)

            def body(s, c):
                if in_z(c, 0):
                    front(s, c)
                if in_z(c, 1):
                    back(s - 1, c - 1)
            pairs_of_steps(pe, body, 1)

        def z_act(act):
            def front(g, gc):
                i = gc % 2
                act.wait_ge(z_ot, g + 1)
                if gc >= 2:
                    act.wait_ge(z_proj, g - 1)
                act.activation(zot[i][:, :], t_bank[:, 0:P], ACT.Copy).then_inc(z_otc, 1)

            def back(g, gc):
                i = gc % 2
                act.wait_ge(z_x1t, g + 1)
                if gc >= 2:
                    act.wait_ge(z_y, g - 1)
                act.activation(zx1t[i][:, :], n_bank[:, 0:P], ACT.Copy).then_inc(z_x1c, 1)
                act.wait_ge(z_gate, g * GATE + 2)
                act.activation(zp[i][:, :], zl[i][:, :], ACT.Exp, bias=zm[i][:, :],
                               accum_out=zs[i][:, 0:1]).then_inc(z_exp, 1)
                act.wait_ge(z_gt, g + 1)
                if gc >= 2:
                    act.wait_ge(z_yb, g - 1)
                act.activation(zgt[i][:, :], n_bank[0:NE, 0:P], ACT.Copy).then_inc(z_gtc, 1)

            def body(s, c):
                if in_z(c, 0):
                    front(s, c)
                if in_z(c, 1):
                    back(s - 1, c - 1)
            pairs_of_steps(act, body, 1)

        def z_dve(dve):
            def front(g, gc):
                i = gc % 2
                dve.wait_ge(z_proj, g + 1)
                dve.wait_ge(z_xb, g + 1)
                dve.tensor_tensor(zh[i][:, :], m_bank[:, 0:P], zxb[i][:, :], ALU.add).then_inc(z_h, 1)
                dve.wait_ge(z_h, g * H1 + 1)
                dve.bn_stats(zmv[i][:, 0:6], zh[i][:, :]).then_inc(z_h, 1)
                dve.wait_ge(z_h, g * H1 + 2)
                waits_end(dve, dve_mark)
                dve.bn_aggr(zmv[i][:, 6:8], zmv[i][:, 0:6]).then_inc(z_h, 1)

            def gating(g, gc):
                i = gc % 2
                k = g * GATE
                dve.wait_ge(z_lg, g + 1)
                dve.tensor_tensor(zl[i][:, :], n_bank[:, 0:NE], gbb[:, :], ALU.add).then_inc(z_gate, 1)
                dve.wait_ge(z_gate, k + 1)
                dve.tensor_reduce(zm[i][:, :], zl[i][:, :], AX_X, ALU.max, negate=True).then_inc(z_gate, 1)
                dve.wait_ge(z_exp, g + 1)
                mine = zp[i][:, :].unsqueeze(2).broadcast_to([P, NE, NE])
                other = zp[i][:, :].unsqueeze(1).broadcast_to([P, NE, NE])
                dve.tensor_tensor(zc[i][:, :, :], other, mine, ALU.is_gt).then_inc(z_gate, 1)
                dve.tensor_tensor(zd[i][:, :, :], other, mine, ALU.is_equal).then_inc(z_rank, 1)
                dve.reciprocal(zs[i][:, 1:2], zs[i][:, 0:1]).then_inc(z_rank, 1)
                dve.wait_ge(z_rank, g * 4 + 2)
                dve.tensor_tensor(zd[i][:, :, :], zd[i][:, :, :], lower[:, :, :], ALU.mult).then_inc(z_rank, 1)
                dve.wait_ge(z_rank, g * 4 + 3)
                dve.wait_ge(z_gate, k + 3)
                dve.tensor_tensor(zd[i][:, :, :], zd[i][:, :, :], zc[i][:, :, :], ALU.add).then_inc(z_rank, 1)
                dve.wait_ge(z_rank, g * 4 + 4)
                dve.tensor_reduce(zk[i][:, :], zd[i][:, :, :], AX_X, ALU.add).then_inc(z_gate, 1)
                dve.wait_ge(z_gate, k + 4)
                dve.tensor_scalar(zk[i][:, :], zk[i][:, :], 1.5, zs[i][:, 1:2], ALU.is_lt, ALU.mult).then_inc(z_gate, 1)
                dve.wait_ge(z_gate, k + 5)
                dve.tensor_tensor(zg[i][:, :], zp[i][:, :], zk[i][:, :], ALU.mult).then_inc(z_gate, 2)

            def experts(g, gc):
                i = gc % 2
                k = g * ACC
                banks = s_bank if gc % 2 == 0 else st_bank
                acc = zacc[i]
                dve.wait_ge(z_yb, g + 1)
                dve.tensor_tensor(acc[0][:, :], u_bank[:, 0:P], zx1[i][:, :], ALU.add).then_inc(z_acc, 1)
                dve.wait_ge(z_y, g + 1)
                for e in range(NE):
                    dve.wait_ge(z_acc, k + e + 1)
                    dve.scalar_tensor_tensor(out=acc[(e + 1) % 2][:, :], in0=banks[e // 4][:, (e % 4) * P:(e % 4 + 1) * P],
                                             scalar=zg[i][:, e:e + 1], in1=acc[e % 2][:, :],
                                             op0=ALU.mult, op1=ALU.add).then_inc(z_acc, 1)
                dve.wait_ge(z_acc, k + 9)
                if gc >= 1:
                    dve.wait_ge(z_fin, (g - 1) * FIN + 1)
                dve.bn_stats(stats[:, 0, :], acc[0][:, :]).then_inc(z_acc, 1)
                dve.wait_ge(z_acc, k + 10)
                waits_end(dve, dve_mark)
                dve.bn_aggr(mv[:, 0, :], stats[:, 0, :]).then_inc(z_acc, 1)

            def body(s, c):
                if in_z(c, 1):
                    gating(s - 1, c - 1)
                if in_z(c, 0):
                    front(s, c)
                if in_z(c, 1):
                    experts(s - 1, c - 1)
            pairs_of_steps(dve, body, 1)

        z_rank = sem("z_rank_steps")

        def z_pool(pool):
            def bias(g, gc):
                i = gc % 2
                pool.wait_ge(z_in, (g + 1) * 48)
                if gc >= 2:
                    pool.wait_ge(z_h, (g - 2) * H1 + 1)
                pool.tensor_tensor(zxb[i][:, :], zxn[i][:, :], bob[:, :], ALU.add).then_inc(z_xb, 1)

            def ln1(g, gc):
                i = gc % 2
                pool.wait_ge(z_h, (g + 1) * H1)
                waits_end(pool, pool_mark)
                pool.tensor_scalar(zvr[i][:, 0:1], zmv[i][:, 7:8], EPS, None, ALU.add).then_inc(z_rs, 1)
                pool.wait_ge(z_rs, g * 2 + 1)
                pool.tensor_tensor(zvr[i][:, 1:2], zvr[i][:, 0:1], mhalf[:, 0:1], ALU.pow).then_inc(z_rs, 1)
                pool.wait_ge(z_rs, g * 2 + 2)
                waits_end(pool, pool_mark)
                pool.tensor_scalar(zn[i][:, :], zh[i][:, :], zmv[i][:, 6:7], zvr[i][:, 1:2],
                                   ALU.subtract, ALU.mult).then_inc(z_x1, 1)
                pool.wait_ge(z_x1, g * 3 + 1)
                pool.tensor_tensor(zn[i][:, :], zn[i][:, :], l1w[:, :], ALU.mult).then_inc(z_x1, 1)
                pool.wait_ge(z_x1, g * 3 + 2)
                if gc >= 2:
                    pool.wait_ge(z_acc, (g - 2) * ACC + 1)
                pool.tensor_tensor(zx1[i][:, :], zn[i][:, :], l1b[:, :], ALU.add).then_inc(z_x1, 1)

            def final(g, gc):
                i = gc % 2
                k = g * FIN
                pool.wait_ge(z_acc, (g + 1) * ACC)
                waits_end(pool, pool_mark)
                pool.tensor_scalar(ve[:, 0:1], mv[:, 0, 1:2], EPS, None, ALU.add).then_inc(z_rs2, 1)
                pool.wait_ge(z_rs2, g * 2 + 1)
                pool.tensor_tensor(rstd[:, 0:1], ve[:, 0:1], mhalf[:, 0:1], ALU.pow).then_inc(z_rs2, 1)
                pool.wait_ge(z_rs2, g * 2 + 2)
                waits_end(pool, pool_mark)
                pool.tensor_scalar(zy[i][:, :], zacc[i][0][:, :], mv[:, 0, 0:1], rstd[:, 0:1],
                                   ALU.subtract, ALU.mult).then_inc(z_fin, 1)
                pool.wait_ge(z_fin, k + 1)
                pool.tensor_tensor(zy[i][:, :], zy[i][:, :], l2w[:, :], ALU.mult).then_inc(z_fin, 1)
                pool.wait_ge(z_fin, k + 2)
                pool.tensor_tensor(zy[i][:, :], zy[i][:, :], l2b[:, :], ALU.add).then_inc(z_fin, 1)
                pool.wait_ge(z_fin, k + 3)
                waits_end(pool, pool_mark)
                pool.tensor_scalar(zy[i][:, :], zy[i][:, :], tg[:, 1:2], None, ALU.mult).then_inc(z_fin, 1)
                pool.wait_ge(z_fin, k + 4)
                if gc >= 2:
                    pool.wait_ge(z_out, (g - 1) * 16)
                pool.tensor_tensor(zo[i][:, :], zy[i][:, :], zx2[i][:, :], ALU.add).then_inc(z_fin, 1)

            def body(s, c):
                if in_z(c, 0):
                    bias(s, c)
                    ln1(s, c)
                if in_z(c, 1):
                    final(s - 1, c - 1)
            pairs_of_steps(pool, body, 1)

        block = es.enter_context(nc.Block())

        @block.sync
        def _(sp):
            def row(dst, src):
                n = src.shape[0]
                sp.dma_start(dst, src.rearrange("(o n) -> o n", o=1).broadcast_to([P, n])).then_inc(c_dma, 16)
            for dst, src in ((idf, ident), (idb, identb), (mqk, mask_qk), (mkq, mask_kq), (wq, wq_t), (wk, wk_t),
                             (wv, wv_t), (wo, wo_t), (gwt, gate_t), (ewt, exp_t), (ebs, exp_b),
                             (cost, cos_t), (sint, sin_t)):
                sp.dma_start(dst[:, :], src).then_inc(c_dma, 16)
            for dst, src in ((bqs, bq), (bks, bk)):
                sp.dma_start(dst[:, :], src.rearrange("(n o) -> n o", o=1)).then_inc(c_dma, 16)
            for dst, src in ((bvb, bv), (bob, bo), (gbb, gate_b), (l1w, ln1w), (l1b, ln1b), (l2w, ln2w), (l2b, ln2b)):
                row(dst[:, :], src)
            row(gates[:, 0:1], g_x)
            row(gates[:, 1:2], g_f)
            sp.wait_ge(c_set, 2 * RING + 3)
            sp_phase(sp, SX, False)
            sp_phase(sp, SY, True)
            z_sp(sp)

        @block.gpsimd
        def _(pool):
            pool.wait_ge(c_dma, 16 * NCONST)
            pool.wait_ge(c_set, 2 * RING + 3)
            pool_phase(pool, SX, False)
            pool_phase(pool, SY, True)
            z_pool(pool)

        @block.tensor
        def _(pe):
            pe.wait_ge(c_dma, 16 * NCONST)
            pe.wait_ge(c_set, 2 * RING + 3)
            pe_phase(pe, SX, False)
            pe.wait_ge(SX.norm, B)
            pe.wait_ge(SX.ucopy, B)
            pe_phase(pe, SY, True)
            pe.wait_ge(SY.norm, B)
            pe.wait_ge(SY.ucopy, B)
            z_pe(pe)

        @block.scalar
        def _(act):
            act.wait_ge(c_dma, 16 * NCONST)
            act.activation(tg[:, :], gates[:, :], ACT.Tanh).then_inc(c_tanh, 1)
            act.activation(bqsc[:, :], bqs[:, :], ACT.Copy, scale=SCALE).then_inc(c_tanh, 1)
            act.wait_ge(c_tanh, 2)
            act_phase(act, SX, False)
            act_phase(act, SY, True)
            z_act(act)

        @block.vector
        def _(dve):
            for i in range(RING):
                dve.memset(kst[i][:, :, :], 1.0).then_inc(c_set, 1)
                dve.memset(vaug[i][:, :, :, :], 1.0).then_inc(c_set, 1)
            dve.memset(u_bank[:, :], 0.0).then_inc(c_set, 1)
            dve.memset(mhalf[:, :], -0.5).then_inc(c_set, 1)
            dve.memset(lower[:, :, :], 0.0).then_inc(c_set, 1)
            dve.wait_ge(c_set, 2 * RING + 3)
            for e in range(1, NE):
                last = dve.memset(lower[:, e, 0:e], 1.0)
            last.then_inc(c_low, 1)
            dve.wait_ge(c_low, 1)
            dve.wait_ge(c_tanh, 2)
            dve_phase(dve, SX, False)
            dve_phase(dve, SY, True)
            z_dve(dve)


def kernel(**inputs):
    import ml_dtypes
    import concourse.bacc as _bacc
    from concourse.bass_utils import run_bass_kernel_spmd as _run

    a = {k: np.asarray(v) for k, v in inputs.items()}
    w_in, b_in = a["L0_ffn_in_proj_w"], a["L0_ffn_in_proj_b"]

    def rows_pdc(w):
        return w.reshape((2, 8, D) + w.shape[1:]).swapaxes(1, 2).reshape(w.shape)

    inv_freq = (1.0 / np.float32(10000.0) ** (np.arange(0, D, 2, dtype=np.float32) / np.float32(D))).astype(np.float32)
    angle = np.arange(P, dtype=np.float32)[:, None] * inv_freq[None, :]
    cos_t = np.tile(np.repeat(np.cos(angle), 2, axis=1), (1, H)).astype(np.float32)
    sign = np.tile(np.array([-1.0, 1.0], np.float32), D // 2)
    sin_t = np.tile(np.repeat(np.sin(angle), 2, axis=1) * sign, (1, H)).astype(np.float32)
    eye = np.eye(P, dtype=np.float32)
    later = np.triu(np.ones((P, P), np.float32), 1) * np.float32(MASKED)
    arrays = {
        "x": a["x"], "ctx_in": a["ctx_1024"], "g_x": a["g_xattn"], "g_f": a["g_ffn"],
        "wq_t": rows_pdc(w_in[0:P]).T, "wk_t": rows_pdc(w_in[P:2 * P]).T, "wv_t": w_in[2 * P:].T,
        "wo_t": a["L0_ffn_out_proj_w"].T,
        "bq": rows_pdc(b_in[0:P]), "bk": rows_pdc(b_in[P:2 * P]), "bv": b_in[2 * P:], "bo": a["L0_ffn_out_proj_b"],
        "gate_t": a["L0_ffn_gate_w"].T, "gate_b": a["L0_ffn_gate_b"],
        "exp_t": a["L0_ffn_expert_w"].transpose(2, 0, 1).reshape(P, NE * P), "exp_b": a["L0_ffn_expert_b"],
        "ln1w": a["L0_ffn_ln1_w"], "ln1b": a["L0_ffn_ln1_b"], "ln2w": a["L0_ffn_ln2_w"], "ln2b": a["L0_ffn_ln2_b"],
        "cos_t": cos_t, "sin_t": sin_t, "ident": eye, "identb": eye.astype(ml_dtypes.bfloat16),
        "mask_qk": later.astype(ml_dtypes.bfloat16), "mask_kq": later.T.astype(ml_dtypes.bfloat16),
    }
    nc = _bacc.Bacc("TRN2", target_bir_lowering=False, num_devices=1)
    feed, aps = {}, []
    for name, value in arrays.items():
        value = np.ascontiguousarray(value)
        feed[name] = value
        aps.append(nc.dram_tensor(name, value.shape, mybir.dt.from_np(value.dtype), kind="ExternalInput").ap())
    aps.append(nc.dram_tensor("out", (B, P, P), F32, kind="ExternalOutput").ap())
    gated_block_kernel(nc, *aps)
    return _run(nc, [feed], core_ids=[0]).results[0]["out"]
```

```python
from contextlib import ExitStack

import numpy as np

import concourse.bass as bass
from concourse import mybir

ALU = mybir.AluOpType
ACT = mybir.ActivationFunctionType
AX_X = mybir.AxisListType.X
F32 = mybir.dt.float32
BF16 = mybir.dt.bfloat16

P = 128
B = 32
H = 16
D = P // H
NE = 8
G = 2
GROUPS = B // G
TILES = G * 4
HEADS = 4
RING = 3
PROWS = 64
SROWS = 7 * D
MROWS = SROWS + 3
STACK_DMAS = 8
UNITS = 2 * GROUPS
X_BOUNDS = [0, 1, 2, 4, GROUPS]
EARLY, LATER = 4, 22
LATE = GROUPS - 2
X_LOOP = (4, 13)
Y_LOOP = (GROUPS + 3, UNITS - 1)
Z_LOOP = (4, GROUPS)
SCALE = float(D) ** -0.5
EPS = 1e-5
MASKED = -1e30
TILE_PA = [(0, 0), (1, 0), (0, 1), (1, 1)]


def gated_block_kernel(nc, x, ctx_in, g_x, g_f, wq_t, wk_t, wv_t, wo_t, bq, bk, bv, bo,
                       gate_t, gate_b, exp_t, exp_b, ln1w, ln1b, ln2w, ln2b,
                       cos_t, sin_t, ident, identb, mask_qk, mask_kq, out):
    es = ExitStack()
    with es:
        def sb(name, shape, dt=F32):
            return es.enter_context(nc.sbuf_tensor(name, shape, dt))

        def sem(name):
            return es.enter_context(nc.semaphore(name))

        idf = sb("idf", [P, P])
        idb = sb("idb", [P, P], BF16)
        mqk = sb("mqk", [P, P], BF16)
        mkq = sb("mkq", [P, P], BF16)
        wq = sb("wq", [P, P]); wk = sb("wk", [P, P]); wv = sb("wv", [P, P]); wo = sb("wo", [P, P])
        bqs = sb("bqs", [P, 1]); bks = sb("bks", [P, 1]); bqsc = sb("bqsc", [P, 1])
        bvb = sb("bvb", [P, P]); bob = sb("bob", [1, P]); onerow = sb("onerow", [1, P])
        gwt = sb("gwt", [P, NE]); gbb = sb("gbb", [P, NE])
        ewt = sb("ewt", [P, NE * P]); ebs = sb("ebs", [NE, P])
        l1w = sb("l1w", [P, P]); l1b = sb("l1b", [P, P]); l2w = sb("l2w", [P, P]); l2b = sb("l2b", [P, P])
        l1wc = sb("l1wc", [P, 1]); l1bc = sb("l1bc", [P, 1])
        cost = sb("cost", [P, P]); sint = sb("sint", [P, P])
        gates = sb("gates_in", [P, 2]); tg = sb("tg", [P, 2])
        mhalf = sb("mhalf", [P, G]); lower = sb("lower", [P, NE, NE])
        x_all = sb("x_all", [P, B, P]); c_all = sb("c_all", [P, B, P])
        xn2_all = sb("xn2_all", [P, B, P]); att_all = c_all
        qst = [sb(f"qst{i}", [P, 8, G * P], BF16) for i in range(RING)]
        kst = [sb(f"kst{i}", [P, 8, G * P], BF16) for i in range(RING)]
        part_dram = [nc.dram_tensor(f"parts{i}", [2, 2, 3, D, 8 * G * P], BF16, kind="Internal").ap()
                     for i in range(RING)]
        vaug = [sb(f"vaug{i}", [P, G, H, D + 1]) for i in range(RING)]
        stats = sb("stats", [P, G, 6]); mv = sb("mv", [P, G, 2]); ve = sb("ve", [P, G]); rstd = sb("rstd", [P, G])
        xp = sb("xp", [P, G, P]); cp = sb("cp", [P, G, P])
        xn2 = sb("xn2", [P, G, P]); rc = sb("rc", [P, G, P]); rs = sb("rs", [P, G, P]); xr = sb("xr", [P, G, P])
        txr = sb("txr", [P, 2 * G * P])
        t32 = sb("t32", [P, 2, G * P]); r32 = sb("r32", [P, 2, G * P])
        part = sb("part", [P, 2, 3, G * P], BF16)
        nm = [sb(f"nm{i}", [P, H]) for i in range(G)]
        mr = [sb(f"mr{i}", [P, H]) for i in range(G)]
        mst = [sb(f"mst{i}", [P, 2, 3, 8], BF16) for i in range(G)]
        mts = [sb(f"mts{i}", [48, P], BF16) for i in range(G)]
        pt = [sb(f"pt{i}", [P, HEADS, P]) for i in range(4)]
        us = sb("us", [P, 4, P])
        rec = sb("rec", [P, H]); ao = [sb(f"ao{i}", [P, P]) for i in range(G)]

        def ps(name, shape, dt=F32):
            return es.enter_context(nc.psum_tensor(name, shape, dt))
        s_bank = [ps(f"s_bank{i}", [P, 512]) for i in range(2)]
        st_bank = [ps(f"st_bank{i}", [P, 512]) for i in range(2)]
        u_bank = ps("u_bank", [P, 512])
        t_bank = ps("t_bank", [P, 512])
        n_bank = ps("n_bank", [P, 512])
        m_bank = ps("m_bank", [P, 512])
        m_bank_b = m_bank[:, :].bitcast(BF16)

        c_dma = sem("constants_loaded"); c_set = sem("constants_set"); c_tanh = sem("tanh_ready"); c_low = sem("lower_set")
        c_late = sem("later_constants_loaded"); c_l2 = sem("last_norm_gated"); c_bq = sem("bias_scaled")
        sp_mark = sem("sp_waits_end"); pool_mark = sem("pool_waits_end"); dve_mark = sem("dve_waits_end")
        pe_mark = sem("pe_waits_end"); act_mark = sem("act_waits_end")
        x_in = [sem(f"x_loaded{i}") for i in range(len(X_BOUNDS) - 1)]

        stat = sem("stats"); rstd_s = sem("rstd_steps"); ln = sem("ln_applied"); perm = sem("context_permuted")
        rope = sem("rope_steps"); kept = sem("xn2_kept"); vx = sem("x_values"); vy = sem("y_values")
        tr = sem("transposed"); txr_s = sem("y_inputs_t_copied"); proj = sem("y_qk_projected")
        vproj = sem("y_v_projected"); t32_s = sem("qk_t_copied"); split_s = sem("split_steps")
        pwr = sem("parts_written"); stack = sem("stacks_written"); sc = sem("scores"); mx = sem("maxima")
        msplit = sem("max_split_steps"); mt = sem("max_transposed"); mts_s = sem("max_t_copied")
        mdma = [sem(f"max_rows_written{b}") for b in range(G)]
        st = sem("scores_t"); ex = sem("exponentials"); av_s = sem("av")
        ucopy = sem("u_copied"); ut = sem("u_transposed"); rec_s = sem("reciprocal"); norm = sem("normalised")
        res = sem("x_residual_added")

        def waits_end(eng, mark):
            eng.sem_inc(mark, 1)

        def steps(eng, body):
            def by_hand(a, b):
                for s in range(a, b):
                    body(s, s)

            def loop(a, b):
                with eng.Fori(a, b - RING + 1, RING) as i:
                    for k in range(RING):
                        body(i + k, a + k)
            by_hand(-1, X_LOOP[0])
            loop(*X_LOOP)
            by_hand(X_LOOP[1], Y_LOOP[0])
            loop(*Y_LOOP)
            by_hand(Y_LOOP[1], UNITS + 3)

        def has(c, lag):
            return 0 <= c - lag < UNITS

        def in_y(uc):
            return uc >= GROUPS

        def pair(t, u, uc):
            return t[:, bass.ds((u - (GROUPS if in_y(uc) else 0)) * G, G), :]

        def one(t, u, uc, b):
            return t[:, bass.ds((u - (GROUPS if in_y(uc) else 0)) * G + b, 1), :].rearrange("q o d -> q (o d)")

        def sp_attention(sp):
            def write_parts(u, uc):
                sp.wait_ge(split_s, (u + 1) * 4)
                if uc >= 1:
                    waits_end(sp, sp_mark)
                    sp.wait_ge(stack, u * STACK_DMAS * 16)
                for p in range(2):
                    sp.dma_start(part_dram[uc % RING][p].rearrange("o r d (c t) -> (d c) (o r) t", c=8),
                                 part[PROWS * p:PROWS * (p + 1)].rearrange("p o r t -> p (o r) t")).then_inc(pwr, 16)

            def stacks(u, uc):
                sp.wait_ge(pwr, (u + 1) * 32)
                if uc >= RING:
                    waits_end(sp, sp_mark)
                    sp.wait_ge(st, (u - RING + 1) * TILES)
                z = part_dram[uc % RING].rearrange("p o r d t -> p o (r d) t")
                for stacked, o, parts in ((qst[uc % RING], 0, 2), (kst[uc % RING], 1, 3)):
                    n = parts * D
                    for p in range(2):
                        sp.dma_start(stacked[PROWS * p:PROWS * p + 6 * D].rearrange("r c t -> r (c t)"),
                                     z[p, o, 0:n].unsqueeze(0).broadcast_to([6 * D // n, n, 8 * G * P])
                                     ).then_inc(stack, 16)
                        last = (2 - 2 * o) * D
                        sp.dma_start(stacked[PROWS * p + 6 * D:PROWS * p + 7 * D].rearrange("r c t -> r (c t)"),
                                     z[p, o, last:last + D]).then_inc(stack, 16)

            def max_rows(u, uc, b):
                sp.wait_ge(mts_s, u * G + b + 1)
                for p in range(2):
                    r = PROWS * p + SROWS
                    sp.dma_start(qst[uc % RING][r:r + 3, :, b * P:(b + 1) * P],
                                 mts[b][24 * p:24 * p + 24, :]).then_inc(mdma[b], 16)

            def body(s, c):
                if has(c, 2):
                    max_rows(s - 2, c - 2, 1)
                if has(c, 0):
                    stacks(s, c)
                if has(c, 1):
                    max_rows(s - 1, c - 1, 0)
                if has(c, -1):
                    write_parts(s + 1, c + 1)
            steps(sp, body)

        def rstd_of(pool, v_in, v_eps, r_out, semaphore, k):
            pool.tensor_scalar(v_eps, v_in, 1.0, EPS, ALU.mult, ALU.add).then_inc(semaphore, 1)
            pool.wait_ge(semaphore, k + 1)
            pool.tensor_tensor(r_out, v_eps, mhalf[:, :], ALU.pow).then_inc(semaphore, 1)

        def pool_attention(pool):
            def norm_factor(u, uc):
                pool.wait_ge(stat, (u + 1) * 4)
                if uc >= 1:
                    pool.wait_ge(ln, u * G)
                waits_end(pool, pool_mark)
                rstd_of(pool, mv[:, :, 1], ve[:, :], rstd[:, :], rstd_s, u * 2)

            def rotate(u, uc):
                g = u - GROUPS
                pool.wait_ge(ln, (u + 1) * G)
                pairs = xn2[:, :, :].rearrange("q b (i e) -> q b i e", e=2)
                rot = rs[:, :, :].rearrange("q b (i e) -> q b i e", e=2)
                sg = sint[:, :].rearrange("q (i e) -> q i e", e=2)
                pool.tensor_tensor(rc[:, :, :], xn2[:, :, :], cost[:, :].unsqueeze(1).broadcast_to([P, G, P]),
                                   ALU.mult).then_inc(rope, 1)
                for e in range(2):
                    pool.tensor_tensor(rot[:, :, :, e], pairs[:, :, :, 1 - e],
                                       sg[:, :, e].unsqueeze(1).broadcast_to([P, G, P // 2]),
                                       ALU.mult).then_inc(rope, 1)
                pool.wait_ge(rope, g * 4 + 3)
                pool.wait_ge(tr, u)
                pool.tensor_tensor(xr[:, :, :], rc[:, :, :], rs[:, :, :], ALU.add).then_inc(rope, 1)

            def split_high(u, uc):
                pool.wait_ge(t32_s, (u + 1) * 2)
                if uc >= 1:
                    pool.wait_ge(pwr, u * 32)
                waits_end(pool, pool_mark)
                pool.tensor_scalar(part[:, :, 0, :], t32[:, :, :], 1.0, 0.0, ALU.mult, ALU.add).then_inc(split_s, 1)
                pool.wait_ge(split_s, u * 4 + 1)
                pool.tensor_tensor(r32[:, :, :], t32[:, :, :], part[:, :, 0, :], ALU.subtract).then_inc(split_s, 1)

            def split_low(u, uc):
                pool.wait_ge(split_s, u * 4 + 2)
                waits_end(pool, pool_mark)
                pool.tensor_scalar(part[:, :, 1, :], r32[:, :, :], 1.0, 0.0, ALU.mult, ALU.add).then_inc(split_s, 1)
                pool.wait_ge(split_s, u * 4 + 3)
                pool.tensor_tensor(part[:, :, 2, :], r32[:, :, :], part[:, :, 1, :], ALU.subtract).then_inc(split_s, 1)

            def max_split(u, uc, b):
                k = (u * G + b) * 4
                half = nm[b][:, :].rearrange("q (p c) -> q p c", p=2)
                rest = mr[b][:, :].rearrange("q (p c) -> q p c", p=2)
                pool.wait_ge(mx, u * TILES + 4 * b + 4)
                if uc >= 1:
                    pool.wait_ge(mt, (u - 1) * G + b + 1)
                waits_end(pool, pool_mark)
                pool.tensor_scalar(mst[b][:, :, 0, :], half, 1.0, 0.0, ALU.mult, ALU.add).then_inc(msplit, 1)
                pool.wait_ge(msplit, k + 1)
                pool.tensor_tensor(rest, half, mst[b][:, :, 0, :], ALU.subtract).then_inc(msplit, 1)
                pool.wait_ge(msplit, k + 2)
                waits_end(pool, pool_mark)
                pool.tensor_scalar(mst[b][:, :, 1, :], rest, 1.0, 0.0, ALU.mult, ALU.add).then_inc(msplit, 1)
                pool.wait_ge(msplit, k + 3)
                pool.tensor_tensor(mst[b][:, :, 2, :], rest, mst[b][:, :, 1, :], ALU.subtract).then_inc(msplit, 1)

            def add_residual(u, uc, b):
                pool.wait_ge(norm, u * G + b + 1)
                waits_end(pool, pool_mark)
                row = one(x_all, u, uc, b)
                pool.tensor_tensor(row, row, ao[b][:, :], ALU.add).then_inc(res, 1)

            def body(s, c):
                if has(c, 2):
                    max_split(s - 2, c - 2, 1)
                if has(c, -1):
                    norm_factor(s + 1, c + 1)
                if has(c, 3) and not in_y(c - 3):
                    add_residual(s - 3, c - 3, 1)
                if has(c, -1):
                    if in_y(c + 1):
                        rotate(s + 1, c + 1)
                    split_high(s + 1, c + 1)
                if has(c, 1):
                    max_split(s - 1, c - 1, 0)
                if has(c, -1):
                    split_low(s + 1, c + 1)
                if has(c, 2) and not in_y(c - 2):
                    add_residual(s - 2, c - 2, 0)
            def run(s, c):
                if c == LATE:
                    pool.wait_ge(c_late, 16 * LATER)
                body(s, c)
            steps(pool, run)

        def pe_attention(pe):
            def transpose_inputs(u, uc):
                if uc >= 1:
                    pe.wait_ge(t32_s, u * 2)
                if in_y(uc):
                    pe.wait_ge(rope, (u - GROUPS + 1) * 4)
                    srcs = [xr[:, 0, :], xr[:, 1, :], xn2[:, 0, :], xn2[:, 1, :]]
                else:
                    pe.wait_ge(ln, (u + 1) * G)
                    pe.wait_ge(perm, (u + 1) * G)
                    srcs = [xp[:, 0, :], xp[:, 1, :], cp[:, 0, :], cp[:, 1, :]]
                for i, a in enumerate(srcs):
                    ins = pe.transpose(t_bank[:, i * P:(i + 1) * P], a, idf[:, :])
                ins.then_inc(tr, 1)

            def project(u, uc):
                pe.wait_ge(txr_s, u - GROUPS + 1)
                pe.matmul(t_bank[:, 0:G * P], wq[:, :], txr[:, 0:G * P], start=True, stop=True)
                pe.matmul(t_bank[:, G * P:2 * G * P], wk[:, :], txr[:, 0:G * P],
                          start=True, stop=True).then_inc(proj, 1)

            def project_v(u, uc):
                pe.wait_ge(mts_s, (u - 1) * G)
                for b in range(G):
                    ins = pe.matmul(m_bank[:, b * P:(b + 1) * P], txr[:, (G + b) * P:(G + b + 1) * P], wv[:, :],
                                    start=True, stop=True)
                ins.then_inc(vproj, 1)

            def product(bank, t, uc, lhs, rhs, rows, mask):
                b, (p, a) = t // 4, TILE_PA[t % 4]
                if mask is not None:
                    pe.matmul(bank[:, :], idb[:, :], mask[:, :].unsqueeze(1).broadcast_to([P, HEADS, P]),
                              start=True, stop=False, skip_group_check=True)
                r = PROWS * p
                for j in range(HEADS):
                    ins = pe.matmul(bank[:, j * P:(j + 1) * P],
                                    lhs[uc % RING][r:r + rows, 4 * a + j, b * P:(b + 1) * P],
                                    rhs[uc % RING][r:r + rows, 4 * a + j, b * P:(b + 1) * P],
                                    start=mask is None, stop=True, skip_group_check=mask is not None)
                return ins

            def scores(u, uc, t):
                if t == 0:
                    pe.wait_ge(stack, (u + 1) * STACK_DMAS * 16)
                if uc >= 1 or t >= 2:
                    pe.wait_ge(mx, u * TILES + t - 1)
                product(s_bank[t % 2], t, uc, qst, kst, SROWS, mqk if in_y(uc) else None).then_inc(sc, 1)

            def scores_t(u, uc, t):
                if t % 4 == 0:
                    pe.wait_ge(mdma[t // 4], (u + 1) * 32)
                if uc >= 1 or t >= 2:
                    pe.wait_ge(ex, u * TILES + t - 1)
                product(st_bank[t % 2], t, uc, kst, qst, MROWS, mkq if in_y(uc) else None).then_inc(st, 1)

            def av(u, uc, t):
                b, (p, a) = t // 4, TILE_PA[t % 4]
                pe.wait_ge(ex, u * TILES + t + 1)
                if t == 0:
                    if in_y(uc):
                        pe.wait_ge(vy, u - GROUPS + 1)
                    else:
                        pe.wait_ge(vx, u + 1)
                if t % 4 == 0 and (uc >= 1 or b):
                    pe.wait_ge(ucopy, u * G + b)
                r = 2 * p + a
                for j in range(HEADS):
                    ins = pe.matmul(u_bank[32 * j:32 * j + D + 1, r * P:(r + 1) * P],
                                    vaug[uc % RING][:, b, 4 * r + j, :], pt[t % 4][:, j, :],
                                    start=True, stop=True)
                ins.then_inc(av_s, 1)

            def transpose_max(u, uc, b):
                pe.wait_ge(msplit, (u * G + b + 1) * 4)
                if b == 0 and in_y(uc + 1) and uc + 1 < UNITS:
                    pe.wait_ge(vy, u - GROUPS + 2)
                elif uc >= 1 or b:
                    pe.wait_ge(mts_s, u * G + b)
                waits_end(pe, pe_mark)
                pe.transpose(m_bank_b[0:48, 0:P], mst[b][:, :, :, :].rearrange("q p r c -> q (p r c)"),
                             idb[:, :]).then_inc(mt, 1)

            def transpose_u(u, uc, b):
                pe.wait_ge(ucopy, u * G + b + 1)
                if uc >= 1 or b:
                    pe.wait_ge(norm, u * G + b)
                for r in range(4):
                    ins = pe.transpose(n_bank[:, r * P:(r + 1) * P], us[:, r, :], idf[:, :])
                ins.then_inc(ut, 1)

            def body(s, c):
                for t in range(TILES):
                    if has(c, 1):
                        scores(s - 1, c - 1, t)
                    if has(c, 2):
                        scores_t(s - 2, c - 2, t)
                        if t >= 1:
                            av(s - 2, c - 2, t - 1)
                    if t == 1:
                        if has(c, 2):
                            transpose_max(s - 2, c - 2, 1)
                        if has(c, 3):
                            transpose_u(s - 3, c - 3, 1)
                    if t == 2:
                        if has(c, 0) and in_y(c):
                            project_v(s, c)
                    if t == 3 and has(c, -1):
                        transpose_inputs(s + 1, c + 1)
                    if t == 4 and has(c, -1) and in_y(c + 1):
                        project(s + 1, c + 1)
                    if t == 6:
                        if has(c, 2):
                            transpose_u(s - 2, c - 2, 0)
                        if has(c, 1):
                            transpose_max(s - 1, c - 1, 0)
                if has(c, 2):
                    av(s - 2, c - 2, TILES - 1)
            def run(s, c):
                if c == LATE:
                    pe.wait_ge(c_late, 16 * LATER)
                body(s, c)
            steps(pe, run)

        def act_attention(act):
            def copy_t(u, uc):
                act.wait_ge(tr, u + 1)
                if in_y(uc):
                    if uc > GROUPS:
                        act.wait_ge(vproj, u - GROUPS)
                    act.activation(txr[:, :], t_bank[:, :], ACT.Copy).then_inc(txr_s, 1)
                    return
                if uc >= 1:
                    act.wait_ge(split_s, u * 4)
                act.activation(t32[:, 0, :], t_bank[:, 0:G * P], ACT.Copy, scale=SCALE).then_inc(t32_s, 1)
                act.activation(t32[:, 1, :], t_bank[:, G * P:], ACT.Copy).then_inc(t32_s, 1)

            def copy_qk(u, uc):
                act.wait_ge(split_s, u * 4)
                act.wait_ge(proj, u - GROUPS + 1)
                act.activation(t32[:, 0, :], t_bank[:, 0:G * P], ACT.Identity, bias=bqsc[:, :],
                               scale=SCALE).then_inc(t32_s, 1)
                act.activation(t32[:, 1, :], t_bank[:, G * P:], ACT.Identity, bias=bks[:, :]).then_inc(t32_s, 1)

            def values(u, uc):
                if uc >= RING:
                    act.wait_ge(av_s, (u - RING + 1) * TILES)
                waits_end(act, act_mark)
                act.activation(vaug[uc % RING][:, :, :, 0:D],
                               pair(c_all, u, uc).rearrange("k b (h d) -> k b h d", d=D), ACT.Copy).then_inc(vx, 1)

            def keep(u, uc):
                act.wait_ge(ln, (u + 1) * G)
                waits_end(act, act_mark)
                act.activation(pair(xn2_all, u, uc), xn2[:, :, :], ACT.Copy).then_inc(kept, 1)

            def exp(u, uc, t):
                act.wait_ge(st, u * TILES + t + 1)
                if uc >= 1 or t >= 4:
                    act.wait_ge(av_s, u * TILES + t - 3)
                act.activation(pt[t % 4][:, :, :].rearrange("k j q -> k (j q)"), st_bank[t % 2][:, :],
                               ACT.Exp).then_inc(ex, 1)

            def copy_max(u, uc, b):
                act.wait_ge(mt, u * G + b + 1)
                if uc >= 1:
                    act.wait_ge(mdma[b], u * 32)
                act.activation(mts[b][:, :], m_bank_b[0:48, 0:P], ACT.Copy).then_inc(mts_s, 1)

            def copy_u(u, uc, b):
                act.wait_ge(av_s, u * TILES + 4 * b + 4)
                if uc >= 1 or b:
                    act.wait_ge(ut, u * G + b)
                act.activation(us[:, :, :].rearrange("p r q -> p (r q)"), u_bank[:, :], ACT.Copy).then_inc(ucopy, 1)

            def body(s, c):
                if has(c, 3):
                    copy_u(s - 3, c - 3, 1)
                if has(c, 0) and not in_y(c):
                    values(s, c)
                for t in range(TILES):
                    if has(c, 2):
                        exp(s - 2, c - 2, t)
                    if t == 1 and has(c, 2):
                        copy_max(s - 2, c - 2, 1)
                    if t == 2 and has(c, -1) and in_y(c + 1):
                        keep(s + 1, c + 1)
                    if t == 3 and has(c, -1):
                        copy_t(s + 1, c + 1)
                    if t == 4 and has(c, -1) and in_y(c + 1):
                        copy_qk(s + 1, c + 1)
                    if t == 4 and has(c, 2):
                        copy_u(s - 2, c - 2, 0)
                    if t == 6 and has(c, 1):
                        copy_max(s - 1, c - 1, 0)
            def run(s, c):
                if c == LATE:
                    act.wait_ge(c_late, 16 * LATER)
                    act.activation(bqsc[:, :], bqs[:, :], ACT.Copy, scale=SCALE).then_inc(c_bq, 1)
                    act.wait_ge(c_bq, 1)
                body(s, c)
            steps(act, run)

        def dve_attention(dve):
            def statistics(u, uc):
                if not in_y(uc):
                    if uc in X_BOUNDS[:-1]:
                        dve.wait_ge(x_in[X_BOUNDS.index(uc)], 32)
                else:
                    dve.wait_ge(res, (u - GROUPS + 1) * G)
                if uc >= 1:
                    dve.wait_ge(ln, u * G)
                waits_end(dve, dve_mark)
                for b in range(G):
                    dve.bn_stats(stats[:, b, :], one(x_all, u, uc, b)).then_inc(stat, 1)
                dve.wait_ge(stat, u * 4 + 2)
                waits_end(dve, dve_mark)
                for b in range(G):
                    dve.bn_aggr(mv[:, b, :], stats[:, b, :]).then_inc(stat, 1)
                if not in_y(uc):
                    if uc >= 1:
                        dve.wait_ge(tr, u)
                    waits_end(dve, dve_mark)
                    for b in range(G):
                        dve.tensor_copy(cp[:, b, :].rearrange("k (p d c) -> k p c d", p=2, d=D),
                                        one(c_all, u, uc, b).rearrange("k (p c d) -> k p c d", p=2, d=D)
                                        ).then_inc(perm, 1)

            def apply_norm(u, uc):
                dve.wait_ge(rstd_s, (u + 1) * 2)
                if uc >= 1:
                    dve.wait_ge(tr, u)
                if uc > GROUPS:
                    dve.wait_ge(kept, u - GROUPS)
                    dve.wait_ge(rope, (u - GROUPS) * 4)
                waits_end(dve, dve_mark)
                for b in range(G):
                    row = one(x_all, u, uc, b)
                    dst = xn2[:, b, :]
                    if not in_y(uc):
                        dst = xp[:, b, :].rearrange("q (p d c) -> q p c d", p=2, d=D)
                        row = row.rearrange("q (p c d) -> q p c d", p=2, d=D)
                    dve.tensor_scalar(dst, row, mv[:, b, 0:1], rstd[:, b:b + 1],
                                      ALU.subtract, ALU.mult).then_inc(ln, 1)

            def values(u, uc):
                dve.wait_ge(vproj, u - GROUPS + 1)
                dve.wait_ge(av_s, (u - RING + 1) * TILES)
                dve.tensor_tensor(vaug[uc % RING][:, :, :, 0:D],
                                  m_bank[:, 0:G * P].rearrange("k (b h d) -> k b h d", b=G, d=D),
                                  bvb[:, :].rearrange("k (h d) -> k h d", d=D).unsqueeze(1)
                                  .broadcast_to([P, G, H, D]), ALU.add).then_inc(vy, 1)

            def maxima(u, uc, t):
                b, (p, a) = t // 4, TILE_PA[t % 4]
                dve.wait_ge(sc, u * TILES + t + 1)
                if uc >= 1 and t % 4 == 0:
                    dve.wait_ge(msplit, ((u - 1) * G + b + 1) * 4)
                dve.tensor_reduce(nm[b][:, 8 * p + 4 * a:8 * p + 4 * a + 4],
                                  s_bank[t % 2][:, :].rearrange("q (j k) -> q j k", j=HEADS),
                                  AX_X, ALU.max, negate=True).then_inc(mx, 1)

            def normalise(u, uc, b):
                view = n_bank[:, :].rearrange("q (h w) -> q h w", w=32)
                dve.wait_ge(ut, u * G + b + 1)
                dve.reciprocal(rec[:, :], view[:, :, D]).then_inc(rec_s, 1)
                dve.wait_ge(rec_s, u * G + b + 1)
                rb = rec[:, :].unsqueeze(2).broadcast_to([P, H, D])
                if in_y(uc):
                    waits_end(dve, dve_mark)
                    dve.tensor_tensor(one(att_all, u, uc, b).rearrange("q (h d) -> q h d", d=D),
                                      view[:, :, 0:D], rb, ALU.mult).then_inc(norm, 1)
                else:
                    if uc >= 1:
                        dve.wait_ge(res, (u - 1) * G + b + 1)
                    dve.scalar_tensor_tensor(out=ao[b][:, :].rearrange("q (h d) -> q h d", d=D),
                                             in0=view[:, :, 0:D], scalar=tg[:, 0:1], in1=rb,
                                             op0=ALU.mult, op1=ALU.mult).then_inc(norm, 1)

            def body(s, c):
                for t in range(TILES):
                    if has(c, 1):
                        maxima(s - 1, c - 1, t)
                    if t == 0 and has(c, -1):
                        statistics(s + 1, c + 1)
                    if t == 1 and has(c, 3):
                        normalise(s - 3, c - 3, 1)
                    if t == 2 and has(c, -1):
                        apply_norm(s + 1, c + 1)
                    if t == 3 and has(c, 0) and in_y(c):
                        values(s, c)
                    if t == 7 and has(c, 2):
                        normalise(s - 2, c - 2, 0)
            def run(s, c):
                if c == LATE:
                    dve.wait_ge(c_late, 16 * LATER)
                body(s, c)
            steps(dve, run)

        def two(name, shape):
            return [sb(f"{name}{i}", shape) for i in range(2)]
        W = G * P
        zat = two("z_att", [P, G, P])
        zo_t = two("z_att_t", [P, W])
        zh = two("z_h", [P, G, P])
        zst = two("z_stats", [P, G, 6]); zmv = two("z_mv", [P, G, 2]); zve = two("z_ve", [P, G]); zrs = two("z_rstd", [P, G])
        zn = two("z_n", [P, G, P])
        zw = sb("z_nw", [P, G, P]); zx1 = two("z_x1", [P, G, P])
        zx1t = two("z_x1_t", [P, W])
        zl = sb("z_logit", [P, G, NE]); zm = sb("z_max", [P, G]); zp = sb("z_exps", [P, G, NE])
        zs = sb("z_sum", [P, G]); zr = sb("z_rsum", [P, G])
        zc = sb("z_greater", [P, G, NE, NE]); zd = sb("z_before", [P, G, NE, NE]); zk = sb("z_rank", [P, G, NE])
        zt = sb("z_top", [P, G, NE]); zg = two("z_gates", [P, G, NE]); zgt = two("z_gates_t", [NE, W])
        zacc = [sb(f"z_acc{j}", [P, G, P]) for j in range(2)]
        zst2 = sb("z_stats2_", [P, G, 6]); zmv2 = sb("z_mv2_", [P, G, 2]); zve2 = sb("z_ve2_", [P, G])
        zrs2 = sb("z_rstd2_", [P, G]); zy = sb("z_y2", [P, G, P]); zyw = sb("z_yw", [P, G, P])
        zyb = sb("z_ywb", [P, G, P]); zo = two("z_o", [P, G, P])

        z_at = sem("z_att_copied"); z_ot = sem("z_att_transposed"); z_otc = sem("z_att_t_copied")
        z_proj = sem("z_projected"); z_h = sem("z_ln1_steps"); z_rs = sem("z_rstd_steps")
        z_n = sem("z_normalised"); z_x1 = sem("z_x1_steps")
        z_nt = sem("z_n_transposed"); z_x1c = sem("z_x1_t_copied"); z_lg = sem("z_logits_ready")
        z_gate = sem("z_gate_steps"); z_exp = sem("z_gate_exp"); z_gt = sem("z_gates_transposed")
        z_gtc = sem("z_gates_t_copied"); z_y = sem("z_experts"); z_yb = sem("z_expert_bias")
        z_acc = sem("z_accumulated"); z_rs2 = sem("z_rstd2_steps"); z_y2s = sem("z_normalised2")
        z_fin = sem("z_final_steps"); z_out = sem("z_stored")
        H1 = 1 + 2 * G
        GATE = 12
        ACC = 1 + G * NE + 2 * G
        FIN = 3

        def z_steps(eng, body):
            for s in range(0, Z_LOOP[0]):
                body(s, s)
            with eng.Fori(Z_LOOP[0], Z_LOOP[1] - 1, 2) as i:
                body(i, Z_LOOP[0])
                body(i + 1, Z_LOOP[0] + 1)
            for s in range(Z_LOOP[1], GROUPS + 3):
                body(s, s)

        def in_z(c, lag):
            return 0 <= c - lag < GROUPS

        def zpair(t, g):
            return t[:, bass.ds(g * G, G), :]

        def z_sp(sp):
            def body(s, c):
                if in_z(c, 3):
                    sp.wait_ge(z_fin, (s - 2) * FIN)
                    if c > 3:
                        waits_end(sp, sp_mark)
                        sp.wait_ge(z_out, (s - 3) * 16)
                    waits_end(sp, sp_mark)
                    sp.dma_start(out.rearrange("b s d -> s b d")[:, bass.ds((s - 3) * G, G), :],
                                 zo[(c - 3) % 2][:, :, :]).then_inc(z_out, 16)
            z_steps(sp, body)
            sp.wait_ge(z_out, 16 * GROUPS)

        def z_pe(pe):
            def project(g, gc):
                i = gc % 2
                pe.wait_ge(z_at, g + 1)
                if gc >= 1:
                    pe.wait_ge(z_otc, g)
                for b in range(G):
                    ins = pe.transpose(t_bank[:, b * P:(b + 1) * P], zat[i][:, b, :], idf[:, :])
                ins.then_inc(z_ot, 1)
                pe.wait_ge(z_otc, g + 1)
                if gc >= 1:
                    pe.wait_ge(z_h, (g - 1) * H1 + 1)
                for b in range(G):
                    dst = m_bank[:, b * P:(b + 1) * P]
                    pe.matmul(dst, zo_t[i][:, b * P:(b + 1) * P], wo[:, :], start=True, stop=False)
                    ins = pe.matmul(dst, onerow[:, :], bob[:, :], start=False, stop=True)
                ins.then_inc(z_proj, 1)

            def transpose_n(g, gc):
                i = gc % 2
                pe.wait_ge(z_n, (g + 1) * G)
                if gc >= 1:
                    pe.wait_ge(z_x1c, g)
                for b in range(G):
                    ins = pe.transpose(n_bank[:, b * P:(b + 1) * P], zn[i][:, b, :], idf[:, :])
                ins.then_inc(z_nt, 1)

            def experts(g, gc):
                i = gc % 2
                pe.wait_ge(z_x1c, g + 1)
                if gc >= 1:
                    pe.wait_ge(z_acc, (g - 1) * ACC + 1)
                for b in range(G):
                    ins = pe.matmul(u_bank[:, b * NE:(b + 1) * NE], zx1t[i][:, b * P:(b + 1) * P], gwt[:, :],
                                    start=True, stop=True)
                ins.then_inc(z_lg, 1)
                for k in range(2):
                    if gc >= 1:
                        pe.wait_ge(z_acc, (g - 1) * ACC + 1 + G * 4 * (k + 1))
                    for b in range(G):
                        ins = pe.matmul(e_bank[b][k][:, :], zx1t[i][:, b * P:(b + 1) * P],
                                        ewt[:, k * 512:(k + 1) * 512], start=True, stop=True)
                    ins.then_inc(z_y, 1)

            def expert_bias(g, gc):
                i = gc % 2
                pe.wait_ge(z_gate, (g + 1) * GATE)
                for b in range(G):
                    ins = pe.transpose(u_bank[0:NE, W + b * P:W + (b + 1) * P], zg[i][:, b, :], idf[:, :])
                ins.then_inc(z_gt, 1)
                pe.wait_ge(z_gtc, g + 1)
                for b in range(G):
                    ins = pe.matmul(u_bank[:, b * P:(b + 1) * P], zgt[i][:, b * P:(b + 1) * P], ebs[:, :],
                                    start=True, stop=True)
                ins.then_inc(z_yb, 1)

            def body(s, c):
                if in_z(c, 1):
                    transpose_n(s - 1, c - 1)
                    experts(s - 1, c - 1)
                if in_z(c, 0):
                    project(s, c)
                if in_z(c, 1):
                    expert_bias(s - 1, c - 1)
            z_steps(pe, body)

        def z_act(act):
            def fetch(g, gc):
                i = gc % 2
                if gc >= 2:
                    act.wait_ge(z_ot, g - 1)
                waits_end(act, act_mark)
                act.activation(zat[i][:, :, :], zpair(att_all, g), ACT.Copy).then_inc(z_at, 1)

            def copy_att(g, gc):
                i = gc % 2
                act.wait_ge(z_ot, g + 1)
                if gc >= 2:
                    act.wait_ge(z_proj, g - 1)
                act.activation(zo_t[i][:, :], t_bank[:, 0:W], ACT.Copy).then_inc(z_otc, 1)

            def copy_x1(g, gc):
                i = gc % 2
                act.wait_ge(z_nt, g + 1)
                if gc >= 2:
                    act.wait_ge(z_y, (g - 1) * 2)
                act.activation(zx1t[i][:, :], n_bank[:, 0:W], ACT.Identity, bias=l1bc[:, :],
                               scale=l1wc[:, :]).then_inc(z_x1c, 1)

            def gates_exp(g, gc):
                act.wait_ge(z_gate, g * GATE + 3)
                act.activation(zp[:, :, :], zl[:, :, :], ACT.Exp).then_inc(z_exp, 1)

            def copy_gates(g, gc):
                i = gc % 2
                act.wait_ge(z_gt, g + 1)
                if gc >= 2:
                    act.wait_ge(z_yb, g - 1)
                act.activation(zgt[i][:, :], u_bank[0:NE, W:2 * W], ACT.Copy).then_inc(z_gtc, 1)

            def body(s, c):
                if in_z(c, 1):
                    copy_x1(s - 1, c - 1)
                if in_z(c, 0):
                    fetch(s, c)
                if in_z(c, 1):
                    gates_exp(s - 1, c - 1)
                if in_z(c, 0):
                    copy_att(s, c)
                if in_z(c, 1):
                    copy_gates(s - 1, c - 1)
            z_steps(act, body)

        def z_dve(dve):
            def attention_sum(g, gc):
                i = gc % 2
                dve.wait_ge(z_proj, g + 1)
                waits_end(dve, dve_mark)
                dve.tensor_tensor(zh[i][:, :, :], m_bank[:, 0:W].rearrange("q (b d) -> q b d", b=G),
                                  zpair(xn2_all, g), ALU.add).then_inc(z_h, 1)
                dve.wait_ge(z_h, g * H1 + 1)
                waits_end(dve, dve_mark)
                for b in range(G):
                    dve.bn_stats(zst[i][:, b, :], zh[i][:, b, :]).then_inc(z_h, 1)
                dve.wait_ge(z_h, g * H1 + 1 + G)
                waits_end(dve, dve_mark)
                for b in range(G):
                    dve.bn_aggr(zmv[i][:, b, :], zst[i][:, b, :]).then_inc(z_h, 1)

            def normalise1(g, gc):
                i = gc % 2
                dve.wait_ge(z_rs, (g + 1) * 2)
                if gc >= 2:
                    dve.wait_ge(z_nt, g - 1)
                    dve.wait_ge(z_x1, (g - 2) * 2 + 1)
                for b in range(G):
                    dve.tensor_scalar(zn[i][:, b, :], zh[i][:, b, :], zmv[i][:, b, 0:1], zrs[i][:, b:b + 1],
                                      ALU.subtract, ALU.mult).then_inc(z_n, 1)

            def gating(g, gc):
                i = gc % 2
                k = g * GATE
                per_seq = [P, G, NE]
                dve.wait_ge(z_lg, g + 1)
                dve.tensor_tensor(zl[:, :, :], u_bank[:, 0:G * NE].rearrange("q (b e) -> q b e", b=G),
                                  gbb[:, :].unsqueeze(1).broadcast_to(per_seq), ALU.add).then_inc(z_gate, 1)
                dve.wait_ge(z_gate, k + 1)
                dve.tensor_reduce(zm[:, :], zl[:, :, :], AX_X, ALU.max, negate=True).then_inc(z_gate, 1)
                dve.wait_ge(z_gate, k + 2)
                dve.tensor_tensor(zl[:, :, :], zl[:, :, :], zm[:, :].unsqueeze(2).broadcast_to(per_seq),
                                  ALU.add).then_inc(z_gate, 1)
                dve.wait_ge(z_exp, g + 1)
                for b in range(G):
                    mine = zp[:, b, :].unsqueeze(2).broadcast_to([P, NE, NE])
                    other = zp[:, b, :].unsqueeze(1).broadcast_to([P, NE, NE])
                    dve.tensor_tensor(zc[:, b, :, :], other, mine, ALU.is_gt).then_inc(z_gate, 1)
                    dve.tensor_tensor(zd[:, b, :, :], other, mine, ALU.is_equal).then_inc(z_gate, 1)
                dve.tensor_reduce(zs[:, :], zp[:, :, :], AX_X, ALU.add).then_inc(z_gate, 1)
                dve.wait_ge(z_gate, k + 7)
                dve.tensor_tensor(zd[:, :, :, :], zd[:, :, :, :], lower[:, :, :].unsqueeze(1)
                                  .broadcast_to([P, G, NE, NE]), ALU.mult).then_inc(z_rank, 1)
                dve.wait_ge(z_rank, g * 2 + 1)
                dve.tensor_tensor(zd[:, :, :, :], zd[:, :, :, :], zc[:, :, :, :], ALU.add).then_inc(z_rank, 1)
                dve.wait_ge(z_gate, k + 8)
                dve.reciprocal(zr[:, :], zs[:, :]).then_inc(z_gate, 1)
                dve.wait_ge(z_rank, g * 2 + 2)
                dve.tensor_reduce(zk[:, :, :], zd[:, :, :, :], AX_X, ALU.add).then_inc(z_gate, 1)
                dve.wait_ge(z_gate, k + 10)
                dve.scalar_tensor_tensor(out=zt[:, :, :], in0=zk[:, :, :], scalar=1.5, in1=zp[:, :, :],
                                         op0=ALU.is_lt, op1=ALU.mult).then_inc(z_gate, 1)
                dve.wait_ge(z_gate, k + 11)
                dve.tensor_tensor(zg[i][:, :, :], zt[:, :, :], zr[:, :].unsqueeze(2).broadcast_to(per_seq),
                                  ALU.mult).then_inc(z_gate, 1)

            def experts(g, gc):
                i = gc % 2
                k = g * ACC
                dve.wait_ge(z_yb, g + 1)
                dve.wait_ge(z_x1, (g + 1) * 2)
                if gc >= 1:
                    dve.wait_ge(z_y2s, g * G)
                dve.tensor_tensor(zacc[0][:, :, :], u_bank[:, 0:W].rearrange("q (b d) -> q b d", b=G),
                                  zx1[i][:, :, :], ALU.add).then_inc(z_acc, 1)
                for e in range(NE):
                    if e % 4 == 0:
                        dve.wait_ge(z_y, g * 2 + 1 + e // 4)
                    for b in range(G):
                        dve.wait_ge(z_acc, k + 1 + max(0, (e - 1) * G + b + 1))
                        dve.scalar_tensor_tensor(
                            out=zacc[(e + 1) % 2][:, b, :], in0=e_bank[b][e // 4][:, (e % 4) * P:(e % 4 + 1) * P],
                            scalar=zg[i][:, b, e:e + 1], in1=zacc[e % 2][:, b, :],
                            op0=ALU.mult, op1=ALU.add).then_inc(z_acc, 1)
                dve.wait_ge(z_acc, k + 1 + G * NE)
                waits_end(dve, dve_mark)
                for b in range(G):
                    dve.bn_stats(zst2[:, b, :], zacc[0][:, b, :]).then_inc(z_acc, 1)
                dve.wait_ge(z_acc, k + 1 + G * NE + G)
                waits_end(dve, dve_mark)
                for b in range(G):
                    dve.bn_aggr(zmv2[:, b, :], zst2[:, b, :]).then_inc(z_acc, 1)

            def normalise2(g, gc):
                dve.wait_ge(z_rs2, (g + 1) * 2)
                if gc >= 1:
                    dve.wait_ge(z_fin, (g - 1) * FIN + 1)
                for b in range(G):
                    dve.tensor_scalar(zy[:, b, :], zacc[0][:, b, :], zmv2[:, b, 0:1], zrs2[:, b:b + 1],
                                      ALU.subtract, ALU.mult).then_inc(z_y2s, 1)

            def body(s, c):
                if in_z(c, 2):
                    normalise2(s - 2, c - 2)
                if in_z(c, 1):
                    gating(s - 1, c - 1)
                if in_z(c, 0):
                    attention_sum(s, c)
                if in_z(c, 1):
                    experts(s - 1, c - 1)
                if in_z(c, 0):
                    normalise1(s, c)
            z_steps(dve, body)

        z_rank = sem("z_rank_steps")

        def z_pool(pool):
            def x1(g, gc):
                i = gc % 2
                pool.wait_ge(z_n, (g + 1) * G)
                pool.tensor_tensor(zw[:, :, :], zn[i][:, :, :], l1w[:, :].unsqueeze(1).broadcast_to([P, G, P]),
                                   ALU.mult).then_inc(z_x1, 1)
                pool.wait_ge(z_x1, g * 2 + 1)
                if gc >= 2:
                    pool.wait_ge(z_acc, (g - 2) * ACC + 1)
                pool.tensor_tensor(zx1[i][:, :, :], zw[:, :, :], l1b[:, :].unsqueeze(1).broadcast_to([P, G, P]),
                                   ALU.add).then_inc(z_x1, 1)

            def final(g, gc):
                i = gc % 2
                k = g * FIN
                pool.wait_ge(z_y2s, (g + 1) * G)
                pool.tensor_tensor(zyw[:, :, :], zy[:, :, :], l2w[:, :].unsqueeze(1).broadcast_to([P, G, P]),
                                   ALU.mult).then_inc(z_fin, 1)
                pool.wait_ge(z_fin, k + 1)
                pool.tensor_tensor(zyb[:, :, :], zyw[:, :, :], l2b[:, :].unsqueeze(1).broadcast_to([P, G, P]),
                                   ALU.add).then_inc(z_fin, 1)
                pool.wait_ge(z_fin, k + 2)
                if gc >= 2:
                    pool.wait_ge(z_out, (g - 1) * 16)
                waits_end(pool, pool_mark)
                pool.tensor_tensor(zo[i][:, :, :], zyb[:, :, :], zpair(x_all, g), ALU.add).then_inc(z_fin, 1)

            def factor1(g, gc):
                i = gc % 2
                pool.wait_ge(z_h, (g + 1) * H1)
                if gc >= 2:
                    pool.wait_ge(z_n, (g - 1) * G)
                waits_end(pool, pool_mark)
                rstd_of(pool, zmv[i][:, :, 1], zve[i][:, :], zrs[i][:, :], z_rs, g * 2)

            def factor2(g, gc):
                pool.wait_ge(z_acc, (g + 1) * ACC)
                waits_end(pool, pool_mark)
                rstd_of(pool, zmv2[:, :, 1], zve2[:, :], zrs2[:, :], z_rs2, g * 2)

            def body(s, c):
                if in_z(c, 1):
                    x1(s - 1, c - 1)
                if in_z(c, 2):
                    final(s - 2, c - 2)
                if in_z(c, 0):
                    factor1(s, c)
                if in_z(c, 1):
                    factor2(s - 1, c - 1)
            z_steps(pool, body)

        e_bank = [[s_bank[0], s_bank[1]], [st_bank[0], st_bank[1]]]
        SETS = 2 * RING + 4

        block = es.enter_context(nc.Block())

        @block.sync
        def _(sp):
            def row(dst, src, semaphore):
                n = src.shape[0]
                sp.dma_start(dst, src.rearrange("(o n) -> o n", o=1).broadcast_to([dst.shape[0], n])
                             ).then_inc(semaphore, 16)

            def inputs(i):
                part_of = slice(G * X_BOUNDS[i], G * X_BOUNDS[i + 1])
                for dst, src in ((x_all, x), (c_all, ctx_in)):
                    sp.dma_start(dst[:, part_of, :], src.rearrange("b s d -> s b d")[:, part_of, :]
                                 ).then_inc(x_in[i], 16)
            inputs(0)
            sp.dma_start(idf[:, :], ident).then_inc(c_dma, 16)
            row(gates[:, 0:1], g_x, c_dma)
            row(gates[:, 1:2], g_f, c_dma)
            sp.dma_start(idb[:, :], identb).then_inc(c_dma, 16)
            for i in range(1, len(x_in)):
                inputs(i)
            for dst, src in ((mqk, mask_qk), (mkq, mask_kq), (wq, wq_t), (wk, wk_t),
                             (wv, wv_t), (wo, wo_t), (gwt, gate_t), (ewt, exp_t), (ebs, exp_b),
                             (cost, cos_t), (sint, sin_t)):
                sp.dma_start(dst[:, :], src).then_inc(c_late, 16)
            for dst, src in ((bqs, bq), (bks, bk), (l1wc, ln1w), (l1bc, ln1b)):
                sp.dma_start(dst[:, :], src.rearrange("(n o) -> n o", o=1)).then_inc(c_late, 16)
            for dst, src in ((bvb, bv), (bob, bo), (gbb, gate_b), (l1w, ln1w), (l1b, ln1b), (l2w, ln2w), (l2b, ln2b)):
                row(dst[:, :], src, c_late)
            sp.wait_ge(c_set, SETS)
            sp_attention(sp)
            z_sp(sp)

        @block.gpsimd
        def _(pool):
            pool.wait_ge(c_set, SETS)
            pool_attention(pool)
            for t in (l2w, l2b):
                pool.tensor_scalar(t[:, :], t[:, :], tg[:, 1:2], 0.0, ALU.mult, ALU.add).then_inc(c_l2, 1)
            pool.wait_ge(c_l2, 2)
            z_pool(pool)

        @block.tensor
        def _(pe):
            pe.wait_ge(c_dma, 16 * EARLY)
            pe.wait_ge(c_set, SETS)
            pe_attention(pe)
            pe.wait_ge(norm, G * UNITS)
            pe.wait_ge(mts_s, G * UNITS)
            z_pe(pe)

        @block.scalar
        def _(act):
            act.wait_ge(c_dma, 16 * EARLY)
            act.activation(tg[:, :], gates[:, :], ACT.Tanh).then_inc(c_tanh, 1)
            act.wait_ge(c_set, SETS)
            act_attention(act)
            act.wait_ge(norm, G * UNITS)
            z_act(act)

        @block.vector
        def _(dve):
            for i in range(RING):
                dve.memset(kst[i][:, :, :], 1.0).then_inc(c_set, 1)
                dve.memset(vaug[i][:, :, :, :], 1.0).then_inc(c_set, 1)
            dve.memset(u_bank[:, :], 0.0).then_inc(c_set, 1)
            dve.memset(mhalf[:, :], -0.5).then_inc(c_set, 1)
            dve.memset(onerow[:, :], 1.0).then_inc(c_set, 1)
            dve.memset(lower[:, :, :], 0.0).then_inc(c_set, 1)
            dve.wait_ge(c_set, SETS)
            for e in range(1, NE):
                last = dve.memset(lower[:, e, 0:e], 1.0)
            last.then_inc(c_low, 1)
            dve.wait_ge(c_low, 1)
            dve.wait_ge(c_tanh, 1)
            dve_attention(dve)
            z_dve(dve)


def kernel(**inputs):
    import ml_dtypes
    import concourse.bacc as _bacc
    from concourse.bass_utils import run_bass_kernel_spmd as _run

    a = {k: np.asarray(v) for k, v in inputs.items()}
    w_in, b_in = a["L0_ffn_in_proj_w"], a["L0_ffn_in_proj_b"]

    def rows_pdc(w):
        return w.reshape((2, 8, D) + w.shape[1:]).swapaxes(1, 2).reshape(w.shape)

    inv_freq = (1.0 / np.float32(10000.0) ** (np.arange(0, D, 2, dtype=np.float32) / np.float32(D))).astype(np.float32)
    angle = np.arange(P, dtype=np.float32)[:, None] * inv_freq[None, :]
    cos_t = np.tile(np.repeat(np.cos(angle), 2, axis=1), (1, H)).astype(np.float32)
    sign = np.tile(np.array([-1.0, 1.0], np.float32), D // 2)
    sin_t = np.tile(np.repeat(np.sin(angle), 2, axis=1) * sign, (1, H)).astype(np.float32)
    eye = np.eye(P, dtype=np.float32)
    later = np.triu(np.ones((P, P), np.float32), 1) * np.float32(MASKED)
    arrays = {
        "x": a["x"], "ctx_in": a["ctx_1024"], "g_x": a["g_xattn"], "g_f": a["g_ffn"],
        "wq_t": rows_pdc(w_in[0:P]).T, "wk_t": rows_pdc(w_in[P:2 * P]).T, "wv_t": w_in[2 * P:].T,
        "wo_t": a["L0_ffn_out_proj_w"].T,
        "bq": rows_pdc(b_in[0:P]), "bk": rows_pdc(b_in[P:2 * P]), "bv": b_in[2 * P:], "bo": a["L0_ffn_out_proj_b"],
        "gate_t": a["L0_ffn_gate_w"].T, "gate_b": a["L0_ffn_gate_b"],
        "exp_t": a["L0_ffn_expert_w"].transpose(2, 0, 1).reshape(P, NE * P), "exp_b": a["L0_ffn_expert_b"],
        "ln1w": a["L0_ffn_ln1_w"], "ln1b": a["L0_ffn_ln1_b"], "ln2w": a["L0_ffn_ln2_w"], "ln2b": a["L0_ffn_ln2_b"],
        "cos_t": cos_t, "sin_t": sin_t, "ident": eye, "identb": eye.astype(ml_dtypes.bfloat16),
        "mask_qk": later.astype(ml_dtypes.bfloat16), "mask_kq": later.T.astype(ml_dtypes.bfloat16),
    }
    nc = _bacc.Bacc("TRN2", target_bir_lowering=False, num_devices=1)
    feed, aps = {}, []
    for name, value in arrays.items():
        value = np.ascontiguousarray(value)
        feed[name] = value
        aps.append(nc.dram_tensor(name, value.shape, mybir.dt.from_np(value.dtype), kind="ExternalInput").ap())
    aps.append(nc.dram_tensor("out", (B, P, P), F32, kind="ExternalOutput").ap())
    gated_block_kernel(nc, *aps)
    return _run(nc, [feed], core_ids=[0]).results[0]["out"]
```

```python
from contextlib import ExitStack

import numpy as np

import concourse.bass as bass
from concourse import mybir

ALU = mybir.AluOpType
ACT = mybir.ActivationFunctionType
AX_X = mybir.AxisListType.X
F32 = mybir.dt.float32
BF16 = mybir.dt.bfloat16

P = 128
B = 32
H = 16
D = P // H
NE = 8
HALF = NE // 2
G = 2
GROUPS = B // G
TILES = G * 4
HEADS = 4
RING = 3
PARTS = 3
SLOTS = 7
MAX_ROW = 96
STACK_DMAS = 4
DELAY = 2
AV_DELAY = DELAY + 2
UNITS = 2 * GROUPS
X_BOUNDS = [0, 1, 2, 4, GROUPS]
EARLY, LATER = 4, 22
LAST_PIECES = 3
LATE = GROUPS - 2
X_LOOP = (4, 13)
Y_LOOP = (GROUPS + 3, UNITS - 1)
Z_LOOP = (6, GROUPS - 2)
SCALE = float(D) ** -0.5
EPS = 1e-5
MASKED = -1e30


def gated_block_kernel(nc, x, ctx_in, g_x, g_f, wq_t, wk_t, wv_t, wo_t, bq, bk, bv, bo,
                       gate_t, gate_b, exp_t, exp_b, ln1w, ln1b, ln2w, ln2b,
                       cos_t, sin_t, ident, identb, mask_qk, mask_kq, out):
    es = ExitStack()
    with es:
        def sb(name, shape, dt=F32):
            return es.enter_context(nc.sbuf_tensor(name, shape, dt))

        def sem(name):
            return es.enter_context(nc.semaphore(name))

        idf = sb("idf", [P, P])
        idb = sb("idb", [P, P], BF16); ones = sb("ones", [P, 1])
        mqk = sb("mqk", [P, P], BF16)
        mkq = sb("mkq", [P, P], BF16)
        wq = sb("wq", [P, P]); wk = sb("wk", [P, P]); wv = sb("wv", [P, P]); wo = sb("wo", [P, P])
        bqs = sb("bqs", [P, 1]); bks = sb("bks", [P, 1]); bqsc = sb("bqsc", [P, 1])
        bvb = sb("bvb", [P, P]); bob = sb("bob", [1, P]); onerow = sb("onerow", [1, P])
        gwt = sb("gwt", [P, NE]); gbb = sb("gbb", [P, NE])
        ewt = sb("ewt", [P, NE * P]); ebs = sb("ebs", [NE, P])
        l1w = sb("l1w", [P, P]); l1b = sb("l1b", [P, P]); l2w = sb("l2w", [P, P]); l2b = sb("l2b", [P, P])
        l1wc = sb("l1wc", [P, 1]); l1bc = sb("l1bc", [P, 1])
        cost = sb("cost", [P, P]); sint = sb("sint", [P, P])
        gates = sb("gates_in", [P, 2]); tg = sb("tg", [P, 2])
        mhalf = sb("mhalf", [P, G]); lower = sb("lower", [P, NE, NE])
        x_all = sb("x_all", [P, B, P]); c_all = sb("c_all", [P, B, P])
        xn2_all = sb("xn2_all", [P, B, P]); att_all = c_all
        qst = [sb(f"qst{i}", [P, H, G * P], BF16) for i in range(RING)]
        kst = [sb(f"kst{i}", [P, H, G * P], BF16) for i in range(RING)]
        part_dram = [nc.dram_tensor(f"parts{i}", [2, PARTS, D, H * G * P], BF16, kind="Internal").ap()
                     for i in range(RING)]
        vaug = [sb(f"vaug{i}", [P, G, H, D + 1]) for i in range(RING)]
        stats = sb("stats", [P, G, 6]); mv = sb("mv", [P, G, 2]); ve = sb("ve", [P, G]); rstd = sb("rstd", [P, G])
        xp = sb("xp", [P, G, P]); cp = sb("cp", [P, G, P])
        xn2 = sb("xn2", [P, G, P]); rc = sb("rc", [P, G, P]); rs = sb("rs", [P, G, P]); xr = sb("xr", [P, G, P])
        txr = sb("txr", [P, 2 * G * P])
        t32 = sb("t32", [P, 2, G * P]); r32 = sb("r32", [P, 2, G * P])
        part = sb("part", [P, 2, PARTS, G * P], BF16)
        nm = [sb(f"nm{i}", [P, H]) for i in range(G)]
        mr = [sb(f"mr{i}", [P, H]) for i in range(G)]
        mst = [sb(f"mst{i}", [P, PARTS, H], BF16) for i in range(G)]
        mts = [sb(f"mts{i}", [PARTS * H, P], BF16) for i in range(G)]
        pt = [sb(f"pt{i}", [P, HEADS, P]) for i in range(4)]
        us = sb("us", [P, 4, P])
        rec = [sb(f"rec{i}", [P, H]) for i in range(G)]; ao = [sb(f"ao{i}", [P, P]) for i in range(G)]

        def ps(name, shape, dt=F32):
            return es.enter_context(nc.psum_tensor(name, shape, dt))
        s_bank = [ps(f"s_bank{i}", [P, 512]) for i in range(2)]
        st_bank = [ps(f"st_bank{i}", [P, 512]) for i in range(2)]
        u_bank = [ps(f"u_bank{i}", [P, 512]) for i in range(G)]
        t_bank = ps("t_bank", [P, 512])
        m_bank = ps("m_bank", [P, 512])
        m_bank_b = m_bank[:, :].bitcast(BF16)

        c_dma = sem("constants_loaded"); c_set = sem("constants_set"); c_one = sem("ones_set"); c_tanh = sem("tanh_ready"); c_low = sem("lower_set")
        c_late = sem("later_constants_loaded"); c_l2 = sem("last_norm_gated"); c_bq = sem("bias_scaled")
        sp_mark = sem("sp_waits_end"); pool_mark = sem("pool_waits_end"); dve_mark = sem("dve_waits_end")
        pe_mark = sem("pe_waits_end"); act_mark = sem("act_waits_end")
        x_in = [sem(f"x_loaded{i}") for i in range(len(X_BOUNDS) - 1)]

        stat = sem("stats"); rstd_s = sem("rstd_steps"); ln = sem("ln_applied"); perm = sem("context_permuted")
        rope = sem("rope_steps"); kept = sem("xn2_kept"); vx = sem("x_values"); vy = sem("y_values")
        tr = sem("transposed"); txr_s = sem("y_inputs_t_copied"); proj = sem("y_qk_projected")
        vproj = sem("y_v_projected"); t32_s = sem("qk_t_copied"); split_s = sem("split_steps")
        pwr = sem("parts_written"); stack = sem("stacks_written"); sc = sem("scores"); mx = sem("maxima")
        msplit = sem("max_split_steps"); mt = sem("max_transposed"); mts_s = sem("max_t_copied")
        mdma = [sem(f"max_rows_written{b}") for b in range(G)]
        st = sem("scores_t"); ex = sem("exponentials"); av_s = sem("av")
        ucopy = sem("u_copied"); ut = sem("u_transposed"); rec_s = sem("reciprocal"); norm = sem("normalised")
        res = sem("x_residual_added")

        def waits_end(eng, mark):
            eng.sem_inc(mark, 1)

        def steps(eng, body):
            def by_hand(a, b):
                for s in range(a, b):
                    body(s, s)

            def loop(a, b):
                with eng.Fori(a, b - RING + 1, RING) as i:
                    for k in range(RING):
                        body(i + k, a + k)
            by_hand(-1, X_LOOP[0])
            loop(*X_LOOP)
            by_hand(X_LOOP[1], Y_LOOP[0])
            loop(*Y_LOOP)
            by_hand(Y_LOOP[1], UNITS + 3)

        def has(c, lag):
            return 0 <= c - lag < UNITS

        def in_y(uc):
            return uc >= GROUPS

        def pair(t, u, uc):
            return t[:, bass.ds((u - (GROUPS if in_y(uc) else 0)) * G, G), :]

        def one(t, u, uc, b):
            return t[:, bass.ds((u - (GROUPS if in_y(uc) else 0)) * G + b, 1), :].rearrange("q o d -> q (o d)")

        def row(sp, dst, src, semaphore):
            n = src.shape[0]
            sp.dma_start(dst, src.rearrange("(o n) -> o n", o=1).broadcast_to([dst.shape[0], n])
                         ).then_inc(semaphore, 16)

        def load_inputs(sp, i, k, pieces):
            n = G * (X_BOUNDS[i + 1] - X_BOUNDS[i]) // pieces
            part_of = slice(G * X_BOUNDS[i] + k * n, G * X_BOUNDS[i] + (k + 1) * n)
            for dst, src in ((x_all, x), (c_all, ctx_in)):
                sp.dma_start(dst[:, part_of, :], src.rearrange("b s d -> s b d")[:, part_of, :]
                             ).then_inc(x_in[i], 16)

        def later_constants(sp):
            for dst, src in ((mqk, mask_qk), (mkq, mask_kq), (wq, wq_t), (wk, wk_t),
                             (wv, wv_t), (wo, wo_t), (gwt, gate_t), (ewt, exp_t), (ebs, exp_b),
                             (cost, cos_t), (sint, sin_t)):
                sp.dma_start(dst[:, :], src).then_inc(c_late, 16)
            for dst, src in ((bqs, bq), (bks, bk), (l1wc, ln1w), (l1bc, ln1b)):
                sp.dma_start(dst[:, :], src.rearrange("(n o) -> n o", o=1)).then_inc(c_late, 16)
            for dst, src in ((bvb, bv), (bob, bo), (gbb, gate_b), (l1w, ln1w), (l1b, ln1b), (l2w, ln2w), (l2b, ln2b)):
                row(sp, dst[:, :], src, c_late)

        def sp_attention(sp):
            def write_parts(u, uc):
                sp.wait_ge(split_s, (u + 1) * 4)
                if uc >= 1:
                    waits_end(sp, sp_mark)
                    sp.wait_ge(stack, u * STACK_DMAS * 16)
                sp.dma_start(part_dram[uc % RING].rearrange("o r d (h t) -> (d h) (o r) t", h=H),
                             part[:, :, :, :].rearrange("p o r t -> p (o r) t")).then_inc(pwr, 16)

            def stacks(u, uc):
                sp.wait_ge(pwr, (u + 1) * 16)
                if uc >= RING:
                    waits_end(sp, sp_mark)
                    sp.wait_ge(st, (u - RING + 1) * TILES)
                z = part_dram[uc % RING].rearrange("o r d t -> o (r d) t")
                for stacked, o, parts in ((qst[uc % RING], 0, 2), (kst[uc % RING], 1, 3)):
                    n, six = parts * D, (SLOTS - 1) * D
                    sp.dma_start(stacked[0:six].rearrange("r h t -> r (h t)"),
                                 z[o, 0:n].unsqueeze(0).broadcast_to([six // n, n, H * G * P])).then_inc(stack, 16)
                    last = (2 - 2 * o) * D
                    sp.dma_start(stacked[six:six + D].rearrange("r h t -> r (h t)"),
                                 z[o, last:last + D]).then_inc(stack, 16)

            def max_rows(u, uc, b):
                sp.wait_ge(mts_s, u * G + b + 1)
                sp.dma_start(qst[uc % RING][MAX_ROW:MAX_ROW + PARTS, :, b * P:(b + 1) * P],
                             mts[b][:, :]).then_inc(mdma[b], 16)

            def body(s, c):
                if has(c, 2):
                    max_rows(s - 2, c - 2, 1)
                if has(c, 0) and in_y(c):
                    write_parts(s, c)
                if has(c, 0):
                    stacks(s, c)
                if has(c, 1):
                    max_rows(s - 1, c - 1, 0)
                if has(c, -1) and not in_y(c + 1):
                    write_parts(s + 1, c + 1)
            def run(s, c):
                body(s, c)
                if 0 <= c < LAST_PIECES - 1:
                    load_inputs(sp, len(x_in) - 1, c + 1, LAST_PIECES)
            steps(sp, run)

        def rstd_of(pool, v_in, v_eps, r_out, semaphore, k):
            pool.tensor_scalar(v_eps, v_in, 1.0, EPS, ALU.mult, ALU.add).then_inc(semaphore, 1)
            pool.wait_ge(semaphore, k + 1)
            pool.tensor_tensor(r_out, v_eps, mhalf[:, :], ALU.pow).then_inc(semaphore, 1)

        def pool_attention(pool):
            def norm_factor(u, uc):
                pool.wait_ge(stat, (u + 1) * 4)
                if uc >= 1:
                    pool.wait_ge(ln, u * G)
                waits_end(pool, pool_mark)
                rstd_of(pool, mv[:, :, 1], ve[:, :], rstd[:, :], rstd_s, u * 2)

            def rotate(u, uc):
                g = u - GROUPS
                pool.wait_ge(ln, (u + 1) * G)
                pairs = xn2[:, :, :].rearrange("q b (i e) -> q b i e", e=2)
                rot = rs[:, :, :].rearrange("q b (i e) -> q b i e", e=2)
                sg = sint[:, :].rearrange("q (i e) -> q i e", e=2)
                pool.tensor_tensor(rc[:, :, :], xn2[:, :, :], cost[:, :].unsqueeze(1).broadcast_to([P, G, P]),
                                   ALU.mult).then_inc(rope, 1)
                for e in range(2):
                    pool.tensor_tensor(rot[:, :, :, e], pairs[:, :, :, 1 - e],
                                       sg[:, :, e].unsqueeze(1).broadcast_to([P, G, P // 2]),
                                       ALU.mult).then_inc(rope, 1)
                pool.wait_ge(rope, g * 4 + 3)
                pool.wait_ge(tr, u)
                pool.tensor_tensor(xr[:, :, :], rc[:, :, :], rs[:, :, :], ALU.add).then_inc(rope, 1)

            def rest_of_high(u, uc):
                pool.wait_ge(split_s, u * 4 + 1)
                pool.tensor_tensor(r32[:, :, :], t32[:, :, :], part[:, :, 0, :], ALU.subtract).then_inc(split_s, 1)

            def split_high(u, uc):
                pool.wait_ge(t32_s, (u + 1) * 2)
                if uc >= 1:
                    pool.wait_ge(pwr, u * 16)
                waits_end(pool, pool_mark)
                pool.tensor_scalar(part[:, :, 0, :], t32[:, :, :], 1.0, 0.0, ALU.mult, ALU.add).then_inc(split_s, 1)
                pool.wait_ge(split_s, u * 4 + 1)
                pool.tensor_tensor(r32[:, :, :], t32[:, :, :], part[:, :, 0, :], ALU.subtract).then_inc(split_s, 1)

            def split_low(u, uc):
                pool.wait_ge(split_s, u * 4 + 2)
                waits_end(pool, pool_mark)
                pool.tensor_scalar(part[:, :, 1, :], r32[:, :, :], 1.0, 0.0, ALU.mult, ALU.add).then_inc(split_s, 1)
                pool.wait_ge(split_s, u * 4 + 3)
                pool.tensor_tensor(part[:, :, 2, :], r32[:, :, :], part[:, :, 1, :], ALU.subtract).then_inc(split_s, 1)

            def max_split(u, uc, b):
                k = (u * G + b) * 4
                whole, rest = nm[b][:, :], mr[b][:, :]
                pool.wait_ge(mx, u * TILES + 4 * b + 4)
                if uc >= 1:
                    pool.wait_ge(mt, (u - 1) * G + b + 1)
                waits_end(pool, pool_mark)
                pool.tensor_scalar(mst[b][:, 0, :], whole, 1.0, 0.0, ALU.mult, ALU.add).then_inc(msplit, 1)
                pool.wait_ge(msplit, k + 1)
                pool.tensor_tensor(rest, whole, mst[b][:, 0, :], ALU.subtract).then_inc(msplit, 1)
                pool.wait_ge(msplit, k + 2)
                waits_end(pool, pool_mark)
                pool.tensor_scalar(mst[b][:, 1, :], rest, 1.0, 0.0, ALU.mult, ALU.add).then_inc(msplit, 1)
                pool.wait_ge(msplit, k + 3)
                pool.tensor_tensor(mst[b][:, 2, :], rest, mst[b][:, 1, :], ALU.subtract).then_inc(msplit, 1)

            def add_residual(u, uc, b):
                pool.wait_ge(norm, u * G + b + 1)
                waits_end(pool, pool_mark)
                row = one(x_all, u, uc, b)
                pool.tensor_tensor(row, row, ao[b][:, :], ALU.add).then_inc(res, 1)

            def body(s, c):
                for t in range(TILES):
                    if t == 0 and has(c, 2):
                        max_split(s - 2, c - 2, 1)
                    if t == 1 and has(c, -1):
                        norm_factor(s + 1, c + 1)
                    if t == 2 and has(c, 3) and not in_y(c - 3):
                        add_residual(s - 3, c - 3, 0)
                    if t == 3 and has(c, -1) and in_y(c + 1):
                        rotate(s + 1, c + 1)
                    if t == 4 and has(c, 1):
                        max_split(s - 1, c - 1, 0)
                    if t == 5 and has(c, -1) and not in_y(c + 1):
                        split_high(s + 1, c + 1)
                    if t == 6 and has(c, -1):
                        if in_y(c + 1):
                            rest_of_high(s + 1, c + 1)
                        else:
                            split_low(s + 1, c + 1)
                    if t == 7 and has(c, 3) and not in_y(c - 3):
                        add_residual(s - 3, c - 3, 1)

            def run(s, c):
                if c == LATE:
                    pool.wait_ge(c_late, 16 * LATER)
                body(s, c)
            steps(pool, run)

        def pe_attention(pe):
            def transpose_inputs(u, uc):
                if uc > GROUPS:
                    pe.wait_ge(split_s, (u - 1) * 4 + 1)
                elif uc >= 1:
                    pe.wait_ge(t32_s, u * 2)
                if in_y(uc):
                    pe.wait_ge(rope, (u - GROUPS + 1) * 4)
                    srcs = [xr[:, 0, :], xr[:, 1, :], xn2[:, 0, :], xn2[:, 1, :]]
                else:
                    pe.wait_ge(ln, (u + 1) * G)
                    pe.wait_ge(perm, (u + 1) * G)
                    srcs = [xp[:, 0, :], xp[:, 1, :], cp[:, 0, :], cp[:, 1, :]]
                for i, a in enumerate(srcs):
                    ins = pe.transpose(t_bank[:, i * P:(i + 1) * P], a, idf[:, :])
                ins.then_inc(tr, 1)

            def project(u, uc):
                pe.wait_ge(txr_s, u - GROUPS + 1)
                pe.matmul(t_bank[:, 0:G * P], wq[:, :], txr[:, 0:G * P], start=True, stop=True)
                pe.matmul(t_bank[:, G * P:2 * G * P], wk[:, :], txr[:, 0:G * P],
                          start=True, stop=True).then_inc(proj, 1)

            def project_v(u, uc):
                pe.wait_ge(mts_s, (u - 1) * G)
                for b in range(G):
                    ins = pe.matmul(m_bank[:, b * P:(b + 1) * P], txr[:, (G + b) * P:(G + b + 1) * P], wv[:, :],
                                    start=True, stop=True)
                ins.then_inc(vproj, 1)

            def product(bank, t, uc, keys_first, rows, mask):
                b, r = t // 4, t % 4
                if mask is not None:
                    pe.matmul(bank[:, :], idb[:, :], mask[:, :].unsqueeze(1).broadcast_to([P, HEADS, P]),
                              start=True, stop=False, skip_group_check=True)
                for j in range(HEADS):
                    q = qst[uc % RING][0:rows, HEADS * r + j, b * P:(b + 1) * P]
                    k = kst[uc % RING][0:rows, HEADS * r + j, b * P:(b + 1) * P]
                    ins = pe.matmul(bank[:, j * P:(j + 1) * P], k if keys_first else q, q if keys_first else k,
                                    start=mask is None, stop=True, skip_group_check=mask is not None)
                return ins

            def scores(u, uc, t):
                if t == 0:
                    pe.wait_ge(stack, (u + 1) * STACK_DMAS * 16)
                if uc >= 1 or t >= 2:
                    pe.wait_ge(mx, u * TILES + t - 1)
                product(s_bank[t % 2], t, uc, False, MAX_ROW, mqk if in_y(uc) else None).then_inc(sc, 1)

            def scores_t(u, uc, t):
                if t % 4 == 0:
                    pe.wait_ge(mdma[t // 4], (u + 1) * 16)
                if uc >= 1 or t >= 2:
                    pe.wait_ge(ex, u * TILES + t - 1)
                product(st_bank[t % 2], t, uc, True, P, mkq if in_y(uc) else None).then_inc(st, 1)

            def av(u, uc, t):
                b, r = t // 4, t % 4
                pe.wait_ge(ex, u * TILES + t + 1)
                if t == 0:
                    if in_y(uc):
                        pe.wait_ge(vy, u - GROUPS + 1)
                    else:
                        pe.wait_ge(vx, u + 1)
                if t % 4 == 0 and uc >= 1:
                    pe.wait_ge(norm, (u - 1) * G + b + 1)
                for j in range(HEADS):
                    ins = pe.matmul(u_bank[b][32 * j:32 * j + D + 1, r * P:(r + 1) * P],
                                    vaug[uc % RING][:, b, 4 * r + j, :], pt[t % 4][:, j, :],
                                    start=True, stop=True)
                ins.then_inc(av_s, 1)

            def transpose_max(u, uc, b):
                pe.wait_ge(msplit, (u * G + b + 1) * 4)
                if b == 0 and in_y(uc + 1) and uc + 1 < UNITS:
                    pe.wait_ge(vy, u - GROUPS + 2)
                elif uc >= 1 or b:
                    pe.wait_ge(mts_s, u * G + b)
                waits_end(pe, pe_mark)
                pe.transpose(m_bank_b[0:PARTS * H, 0:P], mst[b][:, :, :].rearrange("q r h -> q (r h)"),
                             idb[:, :]).then_inc(mt, 1)

            def transpose_u(u, uc, b):
                pe.wait_ge(ucopy, u * G + b + 1)
                for r in range(4):
                    ins = pe.transpose(u_bank[b][:, r * P:(r + 1) * P], us[:, r, :], idf[:, :])
                ins.then_inc(ut, 1)

            def body(s, c):
                for t in range(TILES):
                    if has(c, 1):
                        scores(s - 1, c - 1, t)
                    lag, tt = (2, t - DELAY) if t >= DELAY else (3, t - DELAY + TILES)
                    if has(c, lag):
                        scores_t(s - lag, c - lag, tt)
                    lag, tt = (2, t - AV_DELAY) if t >= AV_DELAY else (3, t - AV_DELAY + TILES)
                    if has(c, lag):
                        av(s - lag, c - lag, tt)
                    if t == 1 and has(c, 2):
                        transpose_max(s - 2, c - 2, 1)
                    if t == 2 and has(c, 0) and in_y(c):
                        project_v(s, c)
                    if t == 0 and has(c, 3):
                        transpose_u(s - 3, c - 3, 0)
                    if has(c, -1) and t == (5 if in_y(c + 1) else 3):
                        transpose_inputs(s + 1, c + 1)
                    if has(c, 1) and t == 6:
                        transpose_max(s - 1, c - 1, 0)
                    if t == 6 and has(c, -1) and in_y(c + 1):
                        project(s + 1, c + 1)
                    if t == 6 and has(c, 3):
                        transpose_u(s - 3, c - 3, 1)
            def run(s, c):
                if c == LATE:
                    pe.wait_ge(c_late, 16 * LATER)
                body(s, c)
            steps(pe, run)

        def act_attention(act):
            def copy_t(u, uc):
                act.wait_ge(tr, u + 1)
                if in_y(uc):
                    if uc > GROUPS:
                        act.wait_ge(vproj, u - GROUPS)
                    act.activation(txr[:, :], t_bank[:, :], ACT.Copy).then_inc(txr_s, 1)
                    return
                if uc >= 1:
                    act.wait_ge(split_s, u * 4)
                act.activation(t32[:, 0, :], t_bank[:, 0:G * P], ACT.Copy, scale=SCALE).then_inc(t32_s, 1)
                act.activation(t32[:, 1, :], t_bank[:, G * P:], ACT.Copy).then_inc(t32_s, 1)

            def copy_qk(u, uc):
                act.wait_ge(split_s, u * 4)
                act.wait_ge(proj, u - GROUPS + 1)
                act.activation(t32[:, 0, :], t_bank[:, 0:G * P], ACT.Identity, bias=bqsc[:, :],
                               scale=SCALE).then_inc(t32_s, 1)
                act.activation(t32[:, 1, :], t_bank[:, G * P:], ACT.Identity, bias=bks[:, :]).then_inc(t32_s, 1)
                act.wait_ge(t32_s, (u + 1) * 2)
                act.wait_ge(pwr, u * 16)
                waits_end(act, act_mark)
                act.activation(part[:, :, 0, :], t32[:, :, :], ACT.Copy).then_inc(split_s, 1)

            def middle_part(u, uc):
                act.wait_ge(split_s, u * 4 + 2)
                act.activation(part[:, :, 1, :], r32[:, :, :], ACT.Copy).then_inc(split_s, 1)

            def values(u, uc):
                if uc >= RING:
                    act.wait_ge(av_s, (u - RING + 1) * TILES)
                waits_end(act, act_mark)
                act.activation(vaug[uc % RING][:, :, :, 0:D],
                               pair(c_all, u, uc).rearrange("k b (h d) -> k b h d", d=D), ACT.Copy).then_inc(vx, 1)

            def keep(u, uc):
                act.wait_ge(ln, (u + 1) * G)
                waits_end(act, act_mark)
                act.activation(pair(xn2_all, u, uc), xn2[:, :, :], ACT.Copy).then_inc(kept, 1)

            def exp(u, uc, t):
                act.wait_ge(st, u * TILES + t + 1)
                if uc >= 1 or t >= 4:
                    act.wait_ge(av_s, u * TILES + t - 3)
                act.activation(pt[t % 4][:, :, :].rearrange("k j q -> k (j q)"), st_bank[t % 2][:, :],
                               ACT.Exp).then_inc(ex, 1)

            def copy_max(u, uc, b):
                act.wait_ge(mt, u * G + b + 1)
                if uc >= 1:
                    act.wait_ge(mdma[b], u * 16)
                act.activation(mts[b][:, :], m_bank_b[0:PARTS * H, 0:P], ACT.Copy).then_inc(mts_s, 1)

            def copy_u(u, uc, b):
                act.wait_ge(av_s, u * TILES + 4 * b + 4)
                if uc >= 1 or b:
                    act.wait_ge(ut, u * G + b)
                act.activation(us[:, :, :].rearrange("p r q -> p (r q)"), u_bank[b][:, :], ACT.Copy).then_inc(ucopy, 1)

            def body(s, c):
                for t in range(TILES):
                    lag, tt = (2, t - DELAY) if t >= DELAY else (3, t - DELAY + TILES)
                    if has(c, lag):
                        exp(s - lag, c - lag, tt)
                    if t == 0 and has(c, 0) and in_y(c):
                        middle_part(s, c)
                    if t == 1 and has(c, 2):
                        copy_max(s - 2, c - 2, 1)
                    if t == 3 and has(c, -1) and not in_y(c + 1):
                        copy_t(s + 1, c + 1)
                    if t == 4 and has(c, -1) and in_y(c + 1):
                        keep(s + 1, c + 1)
                    if t == 4 and has(c, 3):
                        copy_u(s - 3, c - 3, 1)
                    if t == 5:
                        if has(c, -1) and in_y(c + 1):
                            copy_t(s + 1, c + 1)
                    if has(c, 1) and t == 6:
                        copy_max(s - 1, c - 1, 0)
                    if t == 6 and has(c, -1) and in_y(c + 1):
                        copy_qk(s + 1, c + 1)
                    if t == 5 and has(c, 0) and not in_y(c):
                        values(s, c)
                    if t == 7 and has(c, 2):
                        copy_u(s - 2, c - 2, 0)
            def run(s, c):
                if c == LATE:
                    act.wait_ge(c_late, 16 * LATER)
                    act.activation(bqsc[:, :], bqs[:, :], ACT.Copy, scale=SCALE).then_inc(c_bq, 1)
                    act.wait_ge(c_bq, 1)
                body(s, c)
            steps(act, run)

        def dve_attention(dve):
            def statistics(u, uc):
                if not in_y(uc):
                    if uc in X_BOUNDS[:-1]:
                        chunk = X_BOUNDS.index(uc)
                        dve.wait_ge(x_in[chunk], 32 * (LAST_PIECES if chunk == len(x_in) - 1 else 1))
                else:
                    dve.wait_ge(res, (u - GROUPS + 1) * G)
                if uc >= 1:
                    dve.wait_ge(ln, u * G)
                waits_end(dve, dve_mark)
                for b in range(G):
                    dve.bn_stats(stats[:, b, :], one(x_all, u, uc, b)).then_inc(stat, 1)
                dve.wait_ge(stat, u * 4 + 2)
                waits_end(dve, dve_mark)
                for b in range(G):
                    dve.bn_aggr(mv[:, b, :], stats[:, b, :]).then_inc(stat, 1)
                if not in_y(uc):
                    if uc >= 1:
                        dve.wait_ge(tr, u)
                    waits_end(dve, dve_mark)
                    for b in range(G):
                        dve.tensor_copy(cp[:, b, :].rearrange("k (d h) -> k h d", d=D),
                                        one(c_all, u, uc, b).rearrange("k (h d) -> k h d", d=D)
                                        ).then_inc(perm, 1)

            def apply_norm(u, uc):
                dve.wait_ge(rstd_s, (u + 1) * 2)
                if uc >= 1:
                    dve.wait_ge(tr, u)
                if uc > GROUPS:
                    dve.wait_ge(kept, u - GROUPS)
                    dve.wait_ge(rope, (u - GROUPS) * 4)
                waits_end(dve, dve_mark)
                for b in range(G):
                    row = one(x_all, u, uc, b)
                    dst = xn2[:, b, :]
                    if not in_y(uc):
                        dst = xp[:, b, :].rearrange("q (d h) -> q h d", d=D)
                        row = row.rearrange("q (h d) -> q h d", d=D)
                    dve.tensor_scalar(dst, row, mv[:, b, 0:1], rstd[:, b:b + 1],
                                      ALU.subtract, ALU.mult).then_inc(ln, 1)

            def values(u, uc):
                dve.wait_ge(vproj, u - GROUPS + 1)
                dve.wait_ge(av_s, (u - RING + 1) * TILES)
                dve.tensor_tensor(vaug[uc % RING][:, :, :, 0:D],
                                  m_bank[:, 0:G * P].rearrange("k (b h d) -> k b h d", b=G, d=D),
                                  bvb[:, :].rearrange("k (h d) -> k h d", d=D).unsqueeze(1)
                                  .broadcast_to([P, G, H, D]), ALU.add).then_inc(vy, 1)

            def last_part(u, uc):
                dve.wait_ge(split_s, u * 4 + 3)
                dve.tensor_tensor(part[:, :, 2, :], r32[:, :, :], part[:, :, 1, :], ALU.subtract).then_inc(split_s, 1)

            def maxima(u, uc, t):
                b, r = t // 4, t % 4
                dve.wait_ge(sc, u * TILES + t + 1)
                if uc >= 1 and t % 4 == 0:
                    dve.wait_ge(msplit, ((u - 1) * G + b + 1) * 4)
                dve.tensor_reduce(nm[b][:, HEADS * r:HEADS * (r + 1)],
                                  s_bank[t % 2][:, :].rearrange("q (j k) -> q j k", j=HEADS),
                                  AX_X, ALU.max, negate=True).then_inc(mx, 1)

            def normalise(u, uc, b):
                view = u_bank[b][:, :].rearrange("q (h w) -> q h w", w=32)
                dve.wait_ge(ut, u * G + b + 1)
                dve.reciprocal(rec[b][:, :], view[:, :, D]).then_inc(rec_s, 1)
                dve.wait_ge(rec_s, u * G + b + 1)
                rb = rec[b][:, :].unsqueeze(2).broadcast_to([P, H, D])
                if in_y(uc):
                    waits_end(dve, dve_mark)
                    dve.tensor_tensor(one(att_all, u, uc, b).rearrange("q (h d) -> q h d", d=D),
                                      view[:, :, 0:D], rb, ALU.mult).then_inc(norm, 1)
                else:
                    if uc >= 1:
                        dve.wait_ge(res, (u - 1) * G + b + 1)
                    dve.scalar_tensor_tensor(out=ao[b][:, :].rearrange("q (h d) -> q h d", d=D),
                                             in0=view[:, :, 0:D], scalar=tg[:, 0:1], in1=rb,
                                             op0=ALU.mult, op1=ALU.mult).then_inc(norm, 1)

            def body(s, c):
                for t in range(TILES):
                    if has(c, 1):
                        maxima(s - 1, c - 1, t)
                    if t == 0 and has(c, -1):
                        statistics(s + 1, c + 1)
                    if t == 1 and has(c, 0) and in_y(c):
                        last_part(s, c)
                    if t == 1 and has(c, 3):
                        normalise(s - 3, c - 3, 0)
                    if t == 1 and has(c, -1):
                        apply_norm(s + 1, c + 1)
                    if t == 4 and has(c, 0) and in_y(c):
                        values(s, c)
                    if t == 6 and has(c, 3):
                        normalise(s - 3, c - 3, 1)
            def run(s, c):
                if c == LATE:
                    dve.wait_ge(c_late, 16 * LATER)
                body(s, c)
            steps(dve, run)

        def two(name, shape):
            return [sb(f"{name}{i}", shape) for i in range(2)]
        W = G * P
        zat = two("z_att", [P, G, P])
        zo_t = two("z_att_t", [P, W])
        zh = two("z_h", [P, G, P])
        zst = two("z_stats", [P, G, 6]); zmv = two("z_mv", [P, G, 2]); zve = two("z_ve", [P, G]); zrs = two("z_rstd", [P, G])
        zn = two("z_n", [P, G, P])
        zw = sb("z_nw", [P, G, P]); zx1 = two("z_x1", [P, G, P])
        zx1t = two("z_x1_t", [P, W])
        zl = sb("z_logit", [P, G, NE]); zm = sb("z_max", [P, G]); zp = sb("z_exps", [P, G, NE])
        zs = sb("z_sum", [P, G]); zr = sb("z_rsum", [P, G])
        zc = sb("z_greater", [P, G, NE, NE]); zd = sb("z_before", [P, G, NE, NE]); zk = sb("z_rank", [P, G, NE])
        zt = sb("z_top", [P, G, NE]); zg = two("z_gates", [P, G, NE]); zgt = two("z_gates_t", [NE, W])
        zacc = [[sb(f"z_acc{i}{j}", [P, G, P]) for j in range(2)] for i in range(2)]
        zst2 = sb("z_stats2_", [P, G, 6]); zmv2 = sb("z_mv2_", [P, G, 2]); zve2 = sb("z_ve2_", [P, G])
        zrs2 = sb("z_rstd2_", [P, G]); zy = sb("z_y2", [P, G, P]); zyw = sb("z_yw", [P, G, P])
        zsum = sb("z_x1_moe", [P, G, P]); zyg = sb("z_gated", [P, G, HALF, P]); zyb = sb("z_ywb", [P, G, P]); zo = two("z_o", [P, G, P])

        z_at = sem("z_att_copied"); z_ot = sem("z_att_transposed"); z_otc = sem("z_att_t_copied")
        z_proj = sem("z_projected"); z_h = sem("z_ln1_steps"); z_rs = sem("z_rstd_steps")
        z_n = sem("z_normalised"); z_x1 = sem("z_x1_steps")
        z_nt = sem("z_n_transposed"); z_x1c = sem("z_x1_t_copied"); z_lg = sem("z_logits_ready")
        z_gate = sem("z_gate_steps"); z_exp = sem("z_gate_exp"); z_gt = sem("z_gates_transposed")
        z_gtc = sem("z_gates_t_copied"); z_y = [sem(f"z_experts{k}") for k in range(2)]; z_yg = sem("z_experts_gated"); z_yb = sem("z_expert_bias")
        z_acc = sem("z_accumulated"); z_all = sem("z_all_summed_steps"); z_rs2 = sem("z_rstd2_steps"); z_y2s = sem("z_normalised2")
        z_fin = sem("z_final_steps"); z_out = sem("z_stored")
        H1 = 1 + 2 * G
        GATE = 12
        ACC = G * HALF
        ALL = 1 + 2 * G
        FIN = 3

        def z_steps(eng, body):
            for s in range(-1, Z_LOOP[0]):
                body(s, s)
            with eng.Fori(Z_LOOP[0], Z_LOOP[1] - 1, 2) as i:
                body(i, Z_LOOP[0])
                body(i + 1, Z_LOOP[0] + 1)
            for s in range(Z_LOOP[1], GROUPS + 5):
                body(s, s)

        def in_z(c, lag):
            return 0 <= c - lag < GROUPS

        def zpair(t, g):
            return t[:, bass.ds(g * G, G), :]

        def z_sp(sp):
            def body(s, c):
                if in_z(c, 4):
                    sp.wait_ge(z_fin, (s - 3) * FIN)
                    if c > 4:
                        waits_end(sp, sp_mark)
                        sp.wait_ge(z_out, (s - 4) * 16)
                    waits_end(sp, sp_mark)
                    sp.dma_start(out.rearrange("b s d -> s b d")[:, bass.ds((s - 4) * G, G), :],
                                 zo[(c - 4) % 2][:, :, :]).then_inc(z_out, 16)
            z_steps(sp, body)
            sp.wait_ge(z_out, 16 * GROUPS)

        def z_pe(pe):
            def transpose_att(g, gc):
                i = gc % 2
                pe.wait_ge(z_at, g + 1)
                if gc >= 2:
                    pe.wait_ge(z_x1c, g - 1)
                for b in range(G):
                    ins = pe.transpose(t_bank[:, b * P:(b + 1) * P], zat[i][:, b, :], idf[:, :])
                ins.then_inc(z_ot, 1)

            def project(g, gc):
                i = gc % 2
                pe.wait_ge(z_otc, g + 1)
                if gc >= 1:
                    pe.wait_ge(z_h, (g - 1) * H1 + 1)
                for b in range(G):
                    dst = m_bank[:, b * P:(b + 1) * P]
                    pe.matmul(dst, zo_t[i][:, b * P:(b + 1) * P], wo[:, :], start=True, stop=False)
                    ins = pe.matmul(dst, onerow[:, :], bob[:, :], start=False, stop=True)
                ins.then_inc(z_proj, 1)

            def transpose_n(g, gc):
                i = gc % 2
                pe.wait_ge(z_n, (g + 1) * G)
                for b in range(G):
                    ins = pe.transpose(t_bank[:, b * P:(b + 1) * P], zn[i][:, b, :], idf[:, :])
                ins.then_inc(z_nt, 1)

            def logits(g, gc):
                i = gc % 2
                pe.wait_ge(z_x1c, g + 1)
                if gc >= 1:
                    pe.wait_ge(z_gate, (g - 1) * GATE + 1)
                for b in range(G):
                    ins = pe.matmul(u_bank[1][:, b * NE:(b + 1) * NE], zx1t[i][:, b * P:(b + 1) * P], gwt[:, :],
                                    start=True, stop=True)
                ins.then_inc(z_lg, 1)

            def experts(g, gc, k):
                i = gc % 2
                if gc >= 1:
                    if k == 0:
                        pe.wait_ge(z_acc, g * ACC)
                    else:
                        pe.wait_ge(z_yg, g)
                for b in range(G):
                    ins = pe.matmul(e_bank[b][k][:, :], zx1t[i][:, b * P:(b + 1) * P],
                                    ewt[:, k * 512:(k + 1) * 512], start=True, stop=True)
                ins.then_inc(z_y[k], 1)

            def gates_t(g, gc):
                i = gc % 2
                pe.wait_ge(z_gate, (g + 1) * GATE)
                if gc >= 1:
                    pe.wait_ge(z_all, (g - 1) * ALL + 1)
                for b in range(G):
                    ins = pe.transpose(u_bank[0][0:NE, W + b * P:W + (b + 1) * P], zg[i][:, b, :], idf[:, :])
                ins.then_inc(z_gt, 1)

            def gated_sum(g, gc):
                i = gc % 2
                pe.wait_ge(z_gtc, g + 1)
                pe.wait_ge(z_yg, g + 1)
                for b in range(G):
                    dst = u_bank[0][:, b * P:(b + 1) * P]
                    pe.matmul(dst, zgt[i][:, b * P:(b + 1) * P], ebs[:, :], start=True, stop=False)
                    for e in range(HALF):
                        ins = pe.matmul(dst, idf[:, :], zyg[:, b, e, :], start=False, stop=e == HALF - 1)
                ins.then_inc(z_yb, 1)

            def body(s, c):
                if in_z(c, 0):
                    transpose_att(s, c)
                if in_z(c, 2):
                    experts(s - 2, c - 2, 1)
                if in_z(c, 0):
                    project(s, c)
                if in_z(c, 1):
                    transpose_n(s - 1, c - 1)
                if in_z(c, 3):
                    gated_sum(s - 3, c - 3)
                if in_z(c, 1):
                    logits(s - 1, c - 1)
                    experts(s - 1, c - 1, 0)
                if in_z(c, 2):
                    gates_t(s - 2, c - 2)
            z_steps(pe, body)

        def z_act(act):
            def fetch(g, gc):
                i = gc % 2
                if gc >= 2:
                    act.wait_ge(z_ot, g - 1)
                waits_end(act, act_mark)
                act.activation(zat[i][:, :, :], zpair(att_all, g), ACT.Copy).then_inc(z_at, 1)

            def copy_att(g, gc):
                i = gc % 2
                act.wait_ge(z_ot, g + 1)
                if gc >= 2:
                    act.wait_ge(z_proj, g - 1)
                act.activation(zo_t[i][:, :], t_bank[:, 0:W], ACT.Copy).then_inc(z_otc, 1)

            def copy_x1(g, gc):
                i = gc % 2
                act.wait_ge(z_nt, g + 1)
                if gc >= 2:
                    act.wait_ge(z_y[1], g - 1)
                act.activation(zx1t[i][:, :], t_bank[:, 0:W], ACT.Identity, bias=l1bc[:, :],
                               scale=l1wc[:, :]).then_inc(z_x1c, 1)

            def gates_exp(g, gc):
                act.wait_ge(z_gate, g * GATE + 3)
                act.activation(zp[:, :, :], zl[:, :, :], ACT.Exp).then_inc(z_exp, 1)

            def copy_gates(g, gc):
                i = gc % 2
                act.wait_ge(z_gt, g + 1)
                if gc >= 2:
                    act.wait_ge(z_yb, g - 1)
                act.activation(zgt[i][:, :], u_bank[0][0:NE, W:2 * W], ACT.Copy).then_inc(z_gtc, 1)

            def gate_experts(g, gc):
                i = gc % 2
                act.wait_ge(z_gate, (g + 1) * GATE)
                act.wait_ge(z_y[1], g + 1)
                if gc >= 1:
                    act.wait_ge(z_yb, g)
                for b in range(G):
                    for e in range(HALF):
                        ins = act.activation(zyg[:, b, e, :], e_bank[b][1][:, e * P:(e + 1) * P], ACT.Copy,
                                             scale=zg[i][:, b, HALF + e:HALF + e + 1])
                ins.then_inc(z_yg, 1)

            def body(s, c):
                if in_z(c, 2):
                    gates_exp(s - 2, c - 2)
                if in_z(c, 0):
                    copy_att(s, c)
                if in_z(c, 1):
                    copy_x1(s - 1, c - 1)
                if in_z(c, -1):
                    fetch(s + 1, c + 1)
                if in_z(c, 2):
                    gate_experts(s - 2, c - 2)
                    copy_gates(s - 2, c - 2)
            z_steps(act, body)

        def z_dve(dve):
            def attention_sum(g, gc):
                i = gc % 2
                dve.wait_ge(z_proj, g + 1)
                waits_end(dve, dve_mark)
                dve.tensor_tensor(zh[i][:, :, :], m_bank[:, 0:W].rearrange("q (b d) -> q b d", b=G),
                                  zpair(xn2_all, g), ALU.add).then_inc(z_h, 1)
                dve.wait_ge(z_h, g * H1 + 1)
                waits_end(dve, dve_mark)
                for b in range(G):
                    dve.bn_stats(zst[i][:, b, :], zh[i][:, b, :]).then_inc(z_h, 1)
                dve.wait_ge(z_h, g * H1 + 1 + G)
                waits_end(dve, dve_mark)
                for b in range(G):
                    dve.bn_aggr(zmv[i][:, b, :], zst[i][:, b, :]).then_inc(z_h, 1)

            def normalise1(g, gc):
                i = gc % 2
                dve.wait_ge(z_rs, (g + 1) * 2)
                if gc >= 2:
                    dve.wait_ge(z_nt, g - 1)
                    dve.wait_ge(z_x1, (g - 2) * 2 + 1)
                for b in range(G):
                    dve.tensor_scalar(zn[i][:, b, :], zh[i][:, b, :], zmv[i][:, b, 0:1], zrs[i][:, b:b + 1],
                                      ALU.subtract, ALU.mult).then_inc(z_n, 1)

            per_seq = [P, G, NE]

            def shift_logits(g, gc):
                k = g * GATE
                dve.wait_ge(z_lg, g + 1)
                dve.tensor_tensor(zl[:, :, :], u_bank[1][:, 0:G * NE].rearrange("q (b e) -> q b e", b=G),
                                  gbb[:, :].unsqueeze(1).broadcast_to(per_seq), ALU.add).then_inc(z_gate, 1)
                dve.wait_ge(z_gate, k + 1)
                dve.tensor_reduce(zm[:, :], zl[:, :, :], AX_X, ALU.max, negate=True).then_inc(z_gate, 1)
                dve.wait_ge(z_gate, k + 2)
                dve.tensor_tensor(zl[:, :, :], zl[:, :, :], zm[:, :].unsqueeze(2).broadcast_to(per_seq),
                                  ALU.add).then_inc(z_gate, 1)

            def gating(g, gc):
                i = gc % 2
                k = g * GATE
                dve.wait_ge(z_exp, g + 1)
                for b in range(G):
                    mine = zp[:, b, :].unsqueeze(2).broadcast_to([P, NE, NE])
                    other = zp[:, b, :].unsqueeze(1).broadcast_to([P, NE, NE])
                    dve.tensor_tensor(zc[:, b, :, :], other, mine, ALU.is_gt).then_inc(z_gate, 1)
                    dve.tensor_tensor(zd[:, b, :, :], other, mine, ALU.is_equal).then_inc(z_gate, 1)
                dve.tensor_reduce(zs[:, :], zp[:, :, :], AX_X, ALU.add).then_inc(z_gate, 1)
                dve.wait_ge(z_gate, k + 7)
                dve.tensor_tensor(zd[:, :, :, :], zd[:, :, :, :], lower[:, :, :].unsqueeze(1)
                                  .broadcast_to([P, G, NE, NE]), ALU.mult).then_inc(z_rank, 1)
                dve.wait_ge(z_rank, g * 2 + 1)
                dve.tensor_tensor(zd[:, :, :, :], zd[:, :, :, :], zc[:, :, :, :], ALU.add).then_inc(z_rank, 1)
                dve.wait_ge(z_gate, k + 8)
                dve.reciprocal(zr[:, :], zs[:, :]).then_inc(z_gate, 1)
                dve.wait_ge(z_rank, g * 2 + 2)
                dve.tensor_reduce(zk[:, :, :], zd[:, :, :, :], AX_X, ALU.add).then_inc(z_gate, 1)
                dve.wait_ge(z_gate, k + 10)
                dve.scalar_tensor_tensor(out=zt[:, :, :], in0=zk[:, :, :], scalar=1.5, in1=zp[:, :, :],
                                         op0=ALU.is_lt, op1=ALU.mult).then_inc(z_gate, 1)
                dve.wait_ge(z_gate, k + 11)
                dve.tensor_tensor(zg[i][:, :, :], zt[:, :, :], zr[:, :].unsqueeze(2).broadcast_to(per_seq),
                                  ALU.mult).then_inc(z_gate, 1)

            def experts(g, gc):
                i = gc % 2
                k = g * ACC
                dve.wait_ge(z_x1, (g + 1) * 2)
                dve.wait_ge(z_gate, (g + 1) * GATE)
                dve.wait_ge(z_y[0], g + 1)
                if gc >= 2:
                    dve.wait_ge(z_all, (g - 2) * ALL + 1)
                for e in range(HALF):
                    for b in range(G):
                        if e >= 1:
                            dve.wait_ge(z_acc, k + (e - 1) * G + b + 1)
                        dve.scalar_tensor_tensor(
                            out=zacc[i][e % 2][:, b, :], in0=e_bank[b][0][:, e * P:(e + 1) * P],
                            scalar=zg[i][:, b, e:e + 1], in1=zacc[i][(e + 1) % 2][:, b, :] if e else zx1[i][:, b, :],
                            op0=ALU.mult, op1=ALU.add).then_inc(z_acc, 1)

            def all_experts(g, gc):
                k = g * ALL
                dve.wait_ge(z_yb, g + 1)
                if gc >= 1:
                    dve.wait_ge(z_y2s, g * G)
                dve.wait_ge(z_acc, (g + 1) * ACC)
                dve.tensor_tensor(zsum[:, :, :], u_bank[0][:, 0:W].rearrange("q (b d) -> q b d", b=G),
                                  zacc[gc % 2][(HALF - 1) % 2][:, :, :], ALU.add).then_inc(z_all, 1)
                dve.wait_ge(z_all, k + 1)
                waits_end(dve, dve_mark)
                for b in range(G):
                    dve.bn_stats(zst2[:, b, :], zsum[:, b, :]).then_inc(z_all, 1)
                dve.wait_ge(z_all, k + 1 + G)
                waits_end(dve, dve_mark)
                for b in range(G):
                    dve.bn_aggr(zmv2[:, b, :], zst2[:, b, :]).then_inc(z_all, 1)

            def normalise2(g, gc):
                dve.wait_ge(z_rs2, (g + 1) * 2)
                if gc >= 1:
                    dve.wait_ge(z_fin, (g - 1) * FIN + 1)
                for b in range(G):
                    dve.tensor_scalar(zy[:, b, :], zsum[:, b, :], zmv2[:, b, 0:1], zrs2[:, b:b + 1],
                                      ALU.subtract, ALU.mult).then_inc(z_y2s, 1)

            def body(s, c):
                if in_z(c, 2):
                    shift_logits(s - 2, c - 2)
                if in_z(c, 1):
                    normalise1(s - 1, c - 1)
                if in_z(c, 4):
                    normalise2(s - 4, c - 4)
                if in_z(c, 2):
                    gating(s - 2, c - 2)
                    experts(s - 2, c - 2)
                if in_z(c, 0):
                    attention_sum(s, c)
                if in_z(c, 3):
                    all_experts(s - 3, c - 3)
            z_steps(dve, body)

        z_rank = sem("z_rank_steps")

        def z_pool(pool):
            def x1(g, gc):
                i = gc % 2
                pool.wait_ge(z_n, (g + 1) * G)
                pool.tensor_tensor(zw[:, :, :], zn[i][:, :, :], l1w[:, :].unsqueeze(1).broadcast_to([P, G, P]),
                                   ALU.mult).then_inc(z_x1, 1)
                pool.wait_ge(z_x1, g * 2 + 1)
                if gc >= 2:
                    pool.wait_ge(z_acc, (g - 2) * ACC + G)
                pool.tensor_tensor(zx1[i][:, :, :], zw[:, :, :], l1b[:, :].unsqueeze(1).broadcast_to([P, G, P]),
                                   ALU.add).then_inc(z_x1, 1)

            def final(g, gc):
                i = gc % 2
                k = g * FIN
                pool.wait_ge(z_y2s, (g + 1) * G)
                pool.tensor_tensor(zyw[:, :, :], zy[:, :, :], l2w[:, :].unsqueeze(1).broadcast_to([P, G, P]),
                                   ALU.mult).then_inc(z_fin, 1)
                pool.wait_ge(z_fin, k + 1)
                pool.tensor_tensor(zyb[:, :, :], zyw[:, :, :], l2b[:, :].unsqueeze(1).broadcast_to([P, G, P]),
                                   ALU.add).then_inc(z_fin, 1)
                pool.wait_ge(z_fin, k + 2)
                if gc >= 2:
                    pool.wait_ge(z_out, (g - 1) * 16)
                waits_end(pool, pool_mark)
                pool.tensor_tensor(zo[i][:, :, :], zyb[:, :, :], zpair(x_all, g), ALU.add).then_inc(z_fin, 1)

            def factor1(g, gc):
                i = gc % 2
                pool.wait_ge(z_h, (g + 1) * H1)
                if gc >= 2:
                    pool.wait_ge(z_n, (g - 1) * G)
                waits_end(pool, pool_mark)
                rstd_of(pool, zmv[i][:, :, 1], zve[i][:, :], zrs[i][:, :], z_rs, g * 2)

            def factor2(g, gc):
                pool.wait_ge(z_all, (g + 1) * ALL)
                waits_end(pool, pool_mark)
                rstd_of(pool, zmv2[:, :, 1], zve2[:, :], zrs2[:, :], z_rs2, g * 2)

            def body(s, c):
                if in_z(c, 4):
                    final(s - 4, c - 4)
                if in_z(c, 1):
                    x1(s - 1, c - 1)
                if in_z(c, 0):
                    factor1(s, c)
                if in_z(c, 3):
                    factor2(s - 3, c - 3)
            z_steps(pool, body)

        e_bank = [[s_bank[0], s_bank[1]], [st_bank[0], st_bank[1]]]
        SETS = 3 * RING + 4

        block = es.enter_context(nc.Block())

        @block.sync
        def _(sp):
            load_inputs(sp, 0, 0, 1)
            sp.dma_start(idf[:, :], ident).then_inc(c_dma, 16)
            row(sp, gates[:, 0:1], g_x, c_dma)
            row(sp, gates[:, 1:2], g_f, c_dma)
            sp.dma_start(idb[:, :], identb).then_inc(c_dma, 16)
            for i in range(1, len(x_in) - 1):
                load_inputs(sp, i, 0, 1)
            load_inputs(sp, len(x_in) - 1, 0, LAST_PIECES)
            later_constants(sp)
            sp.wait_ge(c_set, SETS)
            sp_attention(sp)
            z_sp(sp)

        @block.gpsimd
        def _(pool):
            for i in (0, 2):
                pool.memset(kst[i][:, :, :], 1.0).then_inc(c_set, 1)
            pool_attention(pool)
            for t in (l2w, l2b):
                pool.tensor_scalar(t[:, :], t[:, :], tg[:, 1:2], 0.0, ALU.mult, ALU.add).then_inc(c_l2, 1)
            pool.wait_ge(c_l2, 2)
            z_pool(pool)

        @block.tensor
        def _(pe):
            pe.wait_ge(c_dma, 16 * EARLY)
            pe.wait_ge(c_set, SETS)
            pe_attention(pe)
            pe.wait_ge(norm, G * UNITS)
            pe.wait_ge(mts_s, G * UNITS)
            z_pe(pe)

        @block.scalar
        def _(act):
            act.wait_ge(c_one, 1)
            act.activation(kst[1][:, :, :].rearrange("r h t -> r (h t)"),
                           ones[:, :].broadcast_to([P, H * G * P]), ACT.Copy).then_inc(c_set, 1)
            act.wait_ge(c_dma, 16 * EARLY)
            act.activation(tg[:, :], gates[:, :], ACT.Tanh).then_inc(c_tanh, 1)
            act.activation(qst[1][:, :, :].rearrange("r h t -> r (h t)"),
                           ones[:, :].broadcast_to([P, H * G * P]), ACT.Copy, scale=0.0).then_inc(c_set, 1)
            act.wait_ge(c_set, SETS)
            act_attention(act)
            act.wait_ge(norm, G * UNITS)
            z_act(act)

        @block.vector
        def _(dve):
            dve.memset(ones[:, :], 1.0).then_inc(c_one, 1)
            dve.memset(mhalf[:, :], -0.5).then_inc(c_set, 1)
            dve.memset(onerow[:, :], 1.0).then_inc(c_set, 1)
            dve.memset(lower[:, :, :], 0.0).then_inc(c_low, 1)
            for b in range(G):
                dve.memset(u_bank[b][:, :], 0.0).then_inc(c_set, 1)
            for i in range(RING):
                if i != 1:
                    dve.memset(qst[i][:, :, :], 0.0).then_inc(c_set, 1)
                dve.memset(vaug[i][:, :, :, :], 1.0).then_inc(c_set, 1)
            dve.wait_ge(c_low, 1)
            for e in range(1, NE):
                last = dve.memset(lower[:, e, 0:e], 1.0)
            last.then_inc(c_low, 1)
            dve.wait_ge(c_low, 2)
            dve.wait_ge(c_tanh, 1)
            dve_attention(dve)
            z_dve(dve)


def kernel(**inputs):
    import ml_dtypes
    import concourse.bacc as _bacc
    from concourse.bass_utils import run_bass_kernel_spmd as _run

    a = {k: np.asarray(v) for k, v in inputs.items()}
    w_in, b_in = a["L0_ffn_in_proj_w"], a["L0_ffn_in_proj_b"]

    def rows_dh(w):
        return w.reshape((H, D) + w.shape[1:]).swapaxes(0, 1).reshape(w.shape)

    inv_freq = (1.0 / np.float32(10000.0) ** (np.arange(0, D, 2, dtype=np.float32) / np.float32(D))).astype(np.float32)
    angle = np.arange(P, dtype=np.float32)[:, None] * inv_freq[None, :]
    cos_t = np.tile(np.repeat(np.cos(angle), 2, axis=1), (1, H)).astype(np.float32)
    sign = np.tile(np.array([-1.0, 1.0], np.float32), D // 2)
    sin_t = np.tile(np.repeat(np.sin(angle), 2, axis=1) * sign, (1, H)).astype(np.float32)
    eye = np.eye(P, dtype=np.float32)
    later = np.triu(np.ones((P, P), np.float32), 1) * np.float32(MASKED)
    arrays = {
        "x": a["x"], "ctx_in": a["ctx_1024"], "g_x": a["g_xattn"], "g_f": a["g_ffn"],
        "wq_t": rows_dh(w_in[0:P]).T, "wk_t": rows_dh(w_in[P:2 * P]).T, "wv_t": w_in[2 * P:].T,
        "wo_t": a["L0_ffn_out_proj_w"].T,
        "bq": rows_dh(b_in[0:P]), "bk": rows_dh(b_in[P:2 * P]), "bv": b_in[2 * P:], "bo": a["L0_ffn_out_proj_b"],
        "gate_t": a["L0_ffn_gate_w"].T, "gate_b": a["L0_ffn_gate_b"],
        "exp_t": a["L0_ffn_expert_w"].transpose(2, 0, 1).reshape(P, NE * P), "exp_b": a["L0_ffn_expert_b"],
        "ln1w": a["L0_ffn_ln1_w"], "ln1b": a["L0_ffn_ln1_b"], "ln2w": a["L0_ffn_ln2_w"], "ln2b": a["L0_ffn_ln2_b"],
        "cos_t": cos_t, "sin_t": sin_t, "ident": eye, "identb": eye.astype(ml_dtypes.bfloat16),
        "mask_qk": later.astype(ml_dtypes.bfloat16), "mask_kq": later.T.astype(ml_dtypes.bfloat16),
    }
    nc = _bacc.Bacc("TRN2", target_bir_lowering=False, num_devices=1)
    feed, aps = {}, []
    for name, value in arrays.items():
        value = np.ascontiguousarray(value)
        feed[name] = value
        aps.append(nc.dram_tensor(name, value.shape, mybir.dt.from_np(value.dtype), kind="ExternalInput").ap())
    aps.append(nc.dram_tensor("out", (B, P, P), F32, kind="ExternalOutput").ap())
    gated_block_kernel(nc, *aps)
    return _run(nc, [feed], core_ids=[0]).results[0]["out"]
```
